# Optimizing a Trainium2 kernel written in Bass

```python
import numpy as np
import jax
import jax.numpy as jnp

def _softmax(x, axis=-1):
    return jax.nn.softmax(x, axis=axis)

def _gelu(x):
    return jax.nn.gelu(x, approximate=True)

def _silu(x):
    return jax.nn.silu(x)

def _sigmoid(x):
    return jax.nn.sigmoid(x)

def _layernorm(x, axis=-1, eps=1e-05):
    m = jnp.mean(x, axis=axis, keepdims=True)
    v = jnp.var(x, axis=axis, keepdims=True)
    return (x - m) / jnp.sqrt(v + eps)

def _scatter_add(tgt, idx, src, axis=0):
    return tgt.at[idx].add(src)

def _segment_sum(src, seg, n):
    return jax.ops.segment_sum(src, seg, n)
kernel_name = 'mk_sandwich_d1_jaxref_r8_932626'

def setup_inputs(seed: int=0):
    np.random.seed(seed)
    _w = jnp.asarray

    def _L0_attn_setup():
        import jax, jax.numpy as jnp
        import numpy as np
        IN_FEATURES = 256
        HEAD_NUM = 64
        D = IN_FEATURES // HEAD_NUM
        SCALE = float(np.sqrt(D))
        key = jax.random.key(seed)
        ks = jax.random.split(key, 9)
        F = IN_FEATURES
        x = jax.random.normal(ks[0], (4, 128, F), dtype=jnp.float32)
        w = lambda k: jax.random.normal(k, (F, F), dtype=jnp.float32) * 0.02
        b = lambda k: jax.random.normal(k, (F,), dtype=jnp.float32) * 0.01
        return {'x': x, 'Wq': w(ks[1]), 'bq': b(ks[2]), 'Wk': w(ks[3]), 'bk': b(ks[4]), 'Wv': w(ks[5]), 'bv': b(ks[6]), 'Wo': w(ks[7]), 'bo': b(ks[8])}
    _L0_attn_in = _L0_attn_setup()

    def _L0_ffn_setup():
        import jax, jax.numpy as jnp
        import numpy as np
        D_MODEL = 256
        NUM_TILES = 64
        D_SLICE = D_MODEL // NUM_TILES
        TILES_PER_CLUSTER = 8
        NUM_CLUSTERS = NUM_TILES // TILES_PER_CLUSTER
        GRID = 16
        LN_EPS = 1e-05
        DIMS = (np.arange(NUM_TILES)[:, None] * D_SLICE + np.arange(D_SLICE)[None, :]) % D_MODEL
        DIMS = jnp.asarray(DIMS, dtype=jnp.int32)

        def _forward(x, ln_gamma, ln_beta, spline_bases, spline_slopes, output_scale):
            B, S, D = x.shape
            N = B * S
            mu = jnp.mean(x, axis=-1, keepdims=True)
            var = jnp.mean(jnp.square(x - mu), axis=-1, keepdims=True)
            xn = (x - mu) * jax.lax.rsqrt(var + LN_EPS) * ln_gamma + ln_beta
            xf = xn.reshape(N, D)
            slope_sign = jnp.sign(jnp.mean(spline_slopes, axis=-1))
            tile_sigs = jnp.zeros((NUM_TILES, D), dtype=x.dtype)
            tile_sigs = tile_sigs.at[jnp.arange(NUM_TILES)[:, None], DIMS].set(slope_sign)
            cluster_sigs = jnp.sign(tile_sigs.reshape(NUM_CLUSTERS, TILES_PER_CLUSTER, D).mean(axis=1))
            cluster_assign = jnp.arange(NUM_TILES, dtype=jnp.int32) // TILES_PER_CLUSTER
            input_sigs = jnp.sign(xf)
            cluster_scores = input_sigs @ cluster_sigs.T
            best_cluster = jnp.argmax(cluster_scores, axis=-1)
            tile_scores = input_sigs @ tile_sigs.T
            in_cluster = cluster_assign[None, :] == best_cluster[:, None]
            tile_idx = jnp.argmax(jnp.where(in_cluster, tile_scores, -jnp.inf), axis=-1)
            tok_dims = DIMS[tile_idx]
            x_slice = jnp.take_along_axis(xf, tok_dims, axis=1)
            tok_min = x_slice.min(axis=1)
            tok_max = x_slice.max(axis=1)
            onehot = tile_idx[None, :] == jnp.arange(NUM_TILES)[:, None]
            tile_min = jnp.where(onehot, tok_min[None, :], jnp.inf).min(axis=1)
            tile_max = jnp.where(onehot, tok_max[None, :], -jnp.inf).max(axis=1)
            mn = tile_min[tile_idx][:, None]
            mx = tile_max[tile_idx][:, None]
            u = jnp.clip((x_slice - mn) / (mx - mn + 1e-08), 0.0, 1.0 - 1e-06)
            gi = jnp.clip((u * GRID).astype(jnp.int32), 0, GRID - 1)
            j = jnp.arange(D_SLICE)[None, :]
            b = spline_bases[tile_idx[:, None], j, gi]
            s = spline_slopes[tile_idx[:, None], j, gi]
            x_local = (u - gi.astype(u.dtype) / GRID) * GRID
            delta = (b + s * x_local) * output_scale[tile_idx][:, None]
            out = jnp.zeros_like(xf).at[jnp.arange(N)[:, None], tok_dims].set(delta)
            return x + out.reshape(B, S, D)
        key = jax.random.key(seed)
        k1, k2, k3, k4, k5, k6 = jax.random.split(key, 6)
        x = jax.random.normal(k1, (4, 512, D_MODEL), dtype=jnp.float32)
        ln_gamma = 1.0 + 0.1 * jax.random.normal(k2, (D_MODEL,), dtype=jnp.float32)
        ln_beta = 0.1 * jax.random.normal(k3, (D_MODEL,), dtype=jnp.float32)
        spline_bases = 0.1 * jax.random.normal(k4, (NUM_TILES, D_SLICE, GRID), dtype=jnp.float32)
        spline_slopes = 0.1 + 0.1 * jax.random.normal(k5, (NUM_TILES, D_SLICE, GRID), dtype=jnp.float32)
        output_scale = 1.0 + 0.1 * jax.random.normal(k6, (NUM_TILES,), dtype=jnp.float32)
        return {'x': x, 'ln_gamma': ln_gamma, 'ln_beta': ln_beta, 'spline_bases': spline_bases, 'spline_slopes': spline_slopes, 'output_scale': output_scale}
    _L0_ffn_in = _L0_ffn_setup()
    _d = {'L0_attn_x': _L0_attn_in['x'], 'L0_attn_Wq': _L0_attn_in['Wq'], 'L0_attn_bq': _L0_attn_in['bq'], 'L0_attn_Wk': _L0_attn_in['Wk'], 'L0_attn_bk': _L0_attn_in['bk'], 'L0_attn_Wv': _L0_attn_in['Wv'], 'L0_attn_bv': _L0_attn_in['bv'], 'L0_attn_Wo': _L0_attn_in['Wo'], 'L0_attn_bo': _L0_attn_in['bo'], 'L0_ffn_ln_gamma': _L0_ffn_in['ln_gamma'], 'L0_ffn_ln_beta': _L0_ffn_in['ln_beta'], 'L0_ffn_spline_bases': _L0_ffn_in['spline_bases'], 'L0_ffn_spline_slopes': _L0_ffn_in['spline_slopes'], 'L0_ffn_output_scale': _L0_ffn_in['output_scale']}
    _x0 = _d['L0_attn_x']
    _d['L0_attn_x'] = jax.random.normal(jax.random.fold_in(jax.random.key(seed), 1), (4, 512, 256), dtype=_x0.dtype)
    del _x0
    return _d

def reference(L0_attn_x, L0_attn_Wq, L0_attn_bq, L0_attn_Wk, L0_attn_bk, L0_attn_Wv, L0_attn_bv, L0_attn_Wo, L0_attn_bo, L0_ffn_ln_gamma, L0_ffn_ln_beta, L0_ffn_spline_bases, L0_ffn_spline_slopes, L0_ffn_output_scale):

    def _L0_attn_ref(x, Wq, bq, Wk, bk, Wv, bv, Wo, bo):
        import jax, jax.numpy as jnp
        import numpy as np
        IN_FEATURES = 256
        HEAD_NUM = 64
        D = IN_FEATURES // HEAD_NUM
        SCALE = float(np.sqrt(D))
        B, S, F = x.shape
        d = D
        h = F // d
        q = x @ Wq + bq
        k = x @ Wk + bk
        v = x @ Wv + bv

        def to_heads(t):
            return t.reshape(B, S, d, h).transpose(0, 2, 1, 3)
        q, k, v = (to_heads(q), to_heads(k), to_heads(v))
        scores = jnp.einsum('bdsh,bdth->bdst', q, k) / SCALE
        weights = jax.nn.softmax(scores, axis=-1)
        feats = jnp.einsum('bdst,bdth->bdsh', weights, v)
        feats = feats.transpose(0, 2, 1, 3).reshape(B, S, F)
        return feats @ Wo + bo

    def _L0_ffn_ref(x, ln_gamma, ln_beta, spline_bases, spline_slopes, output_scale):
        import jax, jax.numpy as jnp
        import numpy as np
        D_MODEL = 256
        NUM_TILES = 64
        D_SLICE = D_MODEL // NUM_TILES
        TILES_PER_CLUSTER = 8
        NUM_CLUSTERS = NUM_TILES // TILES_PER_CLUSTER
        GRID = 16
        LN_EPS = 1e-05
        DIMS = (np.arange(NUM_TILES)[:, None] * D_SLICE + np.arange(D_SLICE)[None, :]) % D_MODEL
        DIMS = jnp.asarray(DIMS, dtype=jnp.int32)

        def _forward(x, ln_gamma, ln_beta, spline_bases, spline_slopes, output_scale):
            B, S, D = x.shape
            N = B * S
            mu = jnp.mean(x, axis=-1, keepdims=True)
            var = jnp.mean(jnp.square(x - mu), axis=-1, keepdims=True)
            xn = (x - mu) * jax.lax.rsqrt(var + LN_EPS) * ln_gamma + ln_beta
            xf = xn.reshape(N, D)
            slope_sign = jnp.sign(jnp.mean(spline_slopes, axis=-1))
            tile_sigs = jnp.zeros((NUM_TILES, D), dtype=x.dtype)
            tile_sigs = tile_sigs.at[jnp.arange(NUM_TILES)[:, None], DIMS].set(slope_sign)
            cluster_sigs = jnp.sign(tile_sigs.reshape(NUM_CLUSTERS, TILES_PER_CLUSTER, D).mean(axis=1))
            cluster_assign = jnp.arange(NUM_TILES, dtype=jnp.int32) // TILES_PER_CLUSTER
            input_sigs = jnp.sign(xf)
            cluster_scores = input_sigs @ cluster_sigs.T
            best_cluster = jnp.argmax(cluster_scores, axis=-1)
            tile_scores = input_sigs @ tile_sigs.T
            in_cluster = cluster_assign[None, :] == best_cluster[:, None]
            tile_idx = jnp.argmax(jnp.where(in_cluster, tile_scores, -jnp.inf), axis=-1)
            tok_dims = DIMS[tile_idx]
            x_slice = jnp.take_along_axis(xf, tok_dims, axis=1)
            tok_min = x_slice.min(axis=1)
            tok_max = x_slice.max(axis=1)
            onehot = tile_idx[None, :] == jnp.arange(NUM_TILES)[:, None]
            tile_min = jnp.where(onehot, tok_min[None, :], jnp.inf).min(axis=1)
            tile_max = jnp.where(onehot, tok_max[None, :], -jnp.inf).max(axis=1)
            mn = tile_min[tile_idx][:, None]
            mx = tile_max[tile_idx][:, None]
            u = jnp.clip((x_slice - mn) / (mx - mn + 1e-08), 0.0, 1.0 - 1e-06)
            gi = jnp.clip((u * GRID).astype(jnp.int32), 0, GRID - 1)
            j = jnp.arange(D_SLICE)[None, :]
            b = spline_bases[tile_idx[:, None], j, gi]
            s = spline_slopes[tile_idx[:, None], j, gi]
            x_local = (u - gi.astype(u.dtype) / GRID) * GRID
            delta = (b + s * x_local) * output_scale[tile_idx][:, None]
            out = jnp.zeros_like(xf).at[jnp.arange(N)[:, None], tok_dims].set(delta)
            return x + out.reshape(B, S, D)
        return _forward(x, ln_gamma, ln_beta, spline_bases, spline_slopes, output_scale)
    x = L0_attn_x
    x = x + _layernorm(_L0_attn_ref(_layernorm(x, axis=-1), L0_attn_Wq, L0_attn_bq, L0_attn_Wk, L0_attn_bk, L0_attn_Wv, L0_attn_bv, L0_attn_Wo, L0_attn_bo), axis=-1)
    x = x + _layernorm(_L0_ffn_ref(_layernorm(x, axis=-1), L0_ffn_ln_gamma, L0_ffn_ln_beta, L0_ffn_spline_bases, L0_ffn_spline_slopes, L0_ffn_output_scale), axis=-1)
    return x

_drawn_inputs = setup_inputs


def setup_inputs(seed=0):
    import zlib

    import numpy as np

    out = dict(_drawn_inputs(seed))
    spreads = {}
    factors = {'L0_attn_bq': 8.0,
     'L0_attn_bk': 8.0,
     'L0_ffn_ln_gamma': 8.0,
     'L0_ffn_ln_beta': 8.0,
     'L0_ffn_spline_bases': 8.0,
     'L0_ffn_spline_slopes': 8.0,
     'L0_ffn_output_scale': 8.0}
    for name, (base, spread) in spreads.items():
        noise = np.random.default_rng([zlib.crc32(name.encode()), seed]).standard_normal(out[name].shape)
        drawn = base * np.exp(spread * noise) if base else spread * noise
        out[name] = jnp.asarray(drawn.astype(out[name].dtype))
    for name, factor in factors.items():
        out[name] = (out[name] * factor).astype(out[name].dtype)
    return out
```

```python
from contextlib import ExitStack

import concourse.bass as bass
from concourse import mybir

F32 = mybir.dt.float32
F32R = mybir.dt.float32r
BF16 = mybir.dt.bfloat16
ALU = mybir.AluOpType
ACT = mybir.ActivationFunctionType
AX = mybir.AxisListType

P = 128
NB, SEQ, F = 4, 512, 256
T = SEQ // P
NT = NB * T
KC = F // P
H, DH = 4, 64
HT = H * T
NTILE, DS, GRID = 64, 4, 16
NCL = 8
EPS = 1e-5
FAR = 1e38
MAGIC = 1.5 * 2.0 ** 23
TW = 2 * DS * GRID + 1 + 2 * DS
TG, TS, TGA, TBE = 0, DS * GRID, 2 * DS * GRID, 2 * DS * GRID + 1
TBT = TBE + DS
CW = P + KC * NTILE + NTILE + GRID

PROLOGUE = [("xt0", 0), ("xt1", 1), ("q0", 0), ("k0", 1), ("v0", 0)]
NEXT_LATE = {"xt0", "xt1", "q0", "k0", "v0"}
POST = {"ft0", "ft1", "o0", "o1", "yt0", "yt1", "key", "oht", "ga0", "ga1"}
SLOTS = {
    3: [("q1", 0)],
    4: [("k1", 1), ("ft0", 0), ("ft1", 1)],
    5: [("v1", 0)],
    6: [("o0", 1), ("o1", 0)],
    8: [("xt0", 1)],
    9: [("xt1", 0)],
    10: [("q0", 1)],
    11: [("yt0", 0), ("yt1", 1)],
    12: [("k0", 0), ("key", 1)],
    13: [("v0", 0)],
    14: [("oht", 1)],
    15: [("ga0", 0), ("ga1", 1)],
}
TAIL = [("ft0", 0), ("ft1", 1), ("o0", 0), ("o1", 1), ("yt0", 0), ("yt1", 1), ("key", 0),
        ("oht", 1), ("ga0", 0), ("ga1", 1)]


def body_fills(first, last):
    return [(n, k) for u in sorted(SLOTS) for n, k in SLOTS[u]
            if not (first and n in POST) and not (last and n in NEXT_LATE)]


def per_bank(fills, bank):
    return sum(1 for _, k in fills if k == bank)


class Phase:

    def __init__(self, b, kind):
        self.b, self.kind = b, kind
        self.first, self.last = kind == "first", kind == "last"
        self.fills = {"prologue": PROLOGUE, "first": body_fills(True, False),
                      "middle": body_fills(False, False), "last": body_fills(False, True),
                      "tail": TAIL}[kind]

    def fill(self, name):
        bank = dict(self.fills)[name]
        at = [n for n, k in self.fills if k == bank].index(name) + 1
        pro, fst = per_bank(PROLOGUE, bank), per_bank(body_fills(True, False), bank)
        mid, lst = per_bank(body_fills(False, False), bank), per_bank(body_fills(False, True), bank)
        if self.kind == "prologue":
            return bank, at
        if self.kind == "first":
            return bank, pro + at
        if self.kind == "middle":
            return bank, mid * (self.b - 1) + pro + fst + at
        if self.kind == "last":
            return bank, pro + fst + mid * (NB - 2) + at
        return bank, pro + fst + mid * (NB - 2) + lst + at


def sandwich(nc, x, wq, bq, wk, bk, wv, bv, wo, bo, gamma, beta, bases, slopes, oscale, consts, out):
    with ExitStack() as ctx:
        def sb(name, shape, dt=F32):
            return ctx.enter_context(nc.sbuf_tensor(name, shape, dt))

        def sem(name):
            return ctx.enter_context(nc.semaphore(name))

        xs_all = sb("x_in", [P, NB, T, F])
        x1 = sb("x1", [P, NB, T, F])
        y = sb("y", [P, NB, T, F])
        xn = sb("xn", [P, T, F])
        xnT = sb("xnT", [P, KC, SEQ])
        W = {n: sb("w" + n, [P, KC, F]) for n in "qkvo"}
        bqk = sb("bqk", [P, 2, KC])
        bqh = sb("bqh", [P, KC])
        bv_rows = sb("bv_rows", [P, F])
        bo_rows = sb("bo_rows", [P, F])
        gbT = sb("gbT", [P, 2, KC])
        cst = sb("cst", [P, CW])
        qT = sb("qT", [P, KC, SEQ])
        kT = sb("kT", [P, KC, SEQ])
        V = sb("V", [P, T, H, DH + 1])
        probs = sb("probs", [P, 4, SEQ])
        probsT = sb("probsT", [P, 4, SEQ])
        nmax = sb("nmax", [P, HT])
        rsum = sb("rsum", [P, H, T])
        feats = sb("feats", [P, T, F])
        featsT = sb("featsT", [P, KC, SEQ])
        attn = sb("attn", [P, T, F])
        attn_n = sb("attn_n", [P, T, F])
        yn = sb("yn", [P, T, F])
        signT = sb("signT", [P, KC, SEQ], BF16)
        route = sb("route", [P, KC, NTILE], BF16)
        slp = sb("slp", [P, KC, GRID])
        ssum = sb("ssum", [P, KC])
        ssgn = sb("ssgn", [P, KC])
        keys = sb("keys", [P, T, NTILE])
        kmax = sb("kmax", [P, T])
        onehot = sb("onehot", [P, NT, NTILE])
        onehotT = sb("onehotT", [NTILE, NB, SEQ])
        table = sb("table", [NTILE, TW])
        G = sb("G", [P, NT, TW])
        pick = sb("pick", [P, T, F])
        far = sb("far", [P, T, NTILE])
        ysl = sb("ysl", [P, NT, DS])
        xsl = sb("xsl", [P, NT, DS])
        tmn = sb("tmn", [P, 2, T])
        acc = sb("acc", [P, 2, NTILE])
        st6 = sb("st6", [P, 3, T, 6])
        mv = sb("mv", [P, 2, T, 2])
        mv1 = sb("mv1", [P, NT, 2])
        rst = sb("rst", [P, 2, T])
        r1 = sb("r1", [P, NT])
        r2 = sb("r2", [P, NT])
        vy = sb("vy", [P, NT])
        tmpv = sb("tmpv", [P, 3, T])
        half = sb("half", [P, NT])
        tmm = sb("tmm", [NTILE, 2])
        lohi = sb("lohi", [P, NT, 2])
        rden = sb("rden", [P, NT])
        u16 = sb("u16", [P, NT, DS])
        gi = sb("gi", [P, NT, DS])
        over = sb("over", [P, NT, DS])
        xloc = sb("xloc", [P, NT, DS])
        piece = sb("piece", [P, NT * DS, GRID])
        hit = sb("hit", [P, NT, 2 * DS, GRID])
        coef = sb("coef", [P, NT, 2 * DS])
        delta = sb("delta", [P, NT, DS])
        sq = sb("sq", [P, NT, DS])
        s1 = sb("s1", [P, NT])
        s2 = sb("s2", [P, NT])
        r3 = sb("r3", [P, NT])
        mr3 = sb("mr3", [P, NT])
        put = sb("put", [P, NB, T, F])
        base = xs_all
        res = sb("res", [P, NB, T, F])

        psS = [ctx.enter_context(nc.psum_tensor(f"psS{i}", [P, SEQ], F32)) for i in range(2)]
        psT = [ctx.enter_context(nc.psum_tensor(f"psT{i}", [P, SEQ], F32)) for i in range(2)]
        psV = [ctx.enter_context(nc.psum_tensor(f"psV{i}", [P, SEQ], F32)) for i in range(2)]
        psX = [ctx.enter_context(nc.psum_tensor(f"psX{i}", [P, SEQ], F32)) for i in range(2)]

        ident = cst[:, 0:P]
        rmask = cst[:, P:P + KC * NTILE].rearrange("p (c n) -> p c n", c=KC)
        tie = cst[:, P + KC * NTILE:P + KC * NTILE + NTILE]
        steps16 = cst[:, P + KC * NTILE + NTILE:CW]

        x_loaded, consts_loaded, bv_loaded = sem("x_loaded"), sem("consts_loaded"), sem("bv_loaded")
        w_loaded = {n: sem("w_loaded_" + n) for n in "qkvo"}
        bqk_loaded, gbT_loaded, slp_loaded = sem("bqk_loaded"), sem("gbT_loaded"), sem("slp_loaded")
        bo_loaded, table_loaded, stored = sem("bo_loaded"), sem("table_loaded"), sem("stored")
        half_set, ones_set = sem("half_set"), sem("ones_set")
        bqh_ready, ssum_ready, ssgn_ready, route_ready = (sem("bqh_ready"), sem("ssum_ready"),
                                                          sem("ssgn_ready"), sem("route_ready"))
        x_stats, x_rstd, xn_ready = sem("x_stats"), sem("x_rstd"), sem("xn_ready")
        filled = [sem("filled0"), sem("filled1")]
        o_copied, key_copied = sem("o_copied"), sem("key_copied")
        xnT_ready, qk_ready, v_ready = sem("xnT_ready"), sem("qk_ready"), sem("v_ready")
        scores_ready, max_ready, probs_ready = sem("scores_ready"), sem("max_ready"), sem("probs_ready")
        turned, turned_act, turned_dve = sem("turned"), sem("turned_act"), sem("turned_dve")
        pv_done, feats_ready, featsT_ready = sem("pv_done"), sem("feats_ready"), sem("featsT_ready")
        a_stats, a_rstd, attn_normed, x1_ready = (sem("a_stats"), sem("a_rstd"), sem("attn_normed"),
                                                  sem("x1_ready"))
        x1_stats, x1_rstd, y_ready, yn_ready = (sem("x1_stats"), sem("x1_rstd"), sem("y_ready"),
                                                sem("yn_ready"))
        sign_ready, onehot_ready, onehotT_ready = (sem("sign_ready"), sem("onehot_ready"),
                                                   sem("onehotT_ready"))
        picked, gathered = sem("picked"), sem("gathered")
        acc_ready, accT_ready, tmm_ready, lohi_filled = (sem("acc_ready"), sem("accT_ready"),
                                                         sem("tmm_ready"), sem("lohi_filled"))
        var3_ready, r3_ready, dr_ready, put_ready, base_ready, res_ready = (
            sem("var3_ready"), sem("r3_ready"), sem("dr_ready"), sem("put_ready"), sem("base_ready"),
            sem("res_ready"))
        dve_chain, pool_chain = sem("dve_chain"), sem("pool_chain")

        def dram_tokens(ap, b):
            return ap[b].rearrange("(p t) f -> p t f", t=T)

        def spread(eng, dst, n):
            return eng.tensor_tensor(dst.rearrange("p (n j) -> p n j", j=DS),
                                     onehot[:, bass.ds(n, 1), :].rearrange("p t n -> p (t n)")
                                     .unsqueeze(2).broadcast_to([P, NTILE, DS]),
                                     delta[:, bass.ds(n, 1), :].broadcast_to([P, NTILE, DS]), ALU.mult)

        block = ctx.enter_context(nc.Block())

        def copied_out(ph, name):
            b = ph.b
            nb = 0 if ph.kind == "prologue" else b + 1
            i = int(name[-1]) if name[-1] in "01" else 0
            return {"xt": (xnT_ready, KC * nb + i + 1),
                    "q0": (qk_ready, 4 * nb + 1), "k0": (qk_ready, 4 * nb + 2),
                    "q1": (qk_ready, 4 * b + 3), "k1": (qk_ready, 4 * b + 4),
                    "v0": (v_ready, 2 * nb + 1), "v1": (v_ready, 2 * b + 2),
                    "ft": (featsT_ready, KC * b - KC + i + 1), "o0": (o_copied, 2 * b - 1),
                    "o1": (o_copied, 2 * b), "yt": (sign_ready, KC * b - KC + i + 1),
                    "ke": (key_copied, b), "oh": (onehotT_ready, b),
                    "ga": (gathered, 2 * b - 2 + i + 1)}[name[:2]]

        def before(ph, name):
            bank = dict(ph.fills)[name]
            mine = [n for n, k in ph.fills if k == bank]
            if name != mine[0]:
                return [copied_out(ph, mine[mine.index(name) - 1])]
            ahead = {"prologue": [], "first": ["prologue"], "middle": ["first" if ph.b == 1 else "middle"],
                     "last": ["middle"], "tail": ["last"]}[ph.kind]
            found = []
            for kind in ahead:
                p = Phase(0 if kind == "prologue" else ph.b - 1, kind)
                last = [n for n, k in p.fills if k == bank][-1]
                found.append(copied_out(p, last))
            return found

        def run(eng, body):
            for b in range(NB):
                body(Phase(b, "first" if b == 0 else "last" if b == NB - 1 else "middle"))

        class Chain:

            def __init__(self, eng, s):
                self.eng, self.s, self.n = eng, s, 0

            def __call__(self, ins):
                self.n += 1
                ins.then_inc(self.s, 1)
                self.eng.wait_ge(self.s, self.n)

        @block.sync
        def _(sp):
            sp.dma_start(xs_all[:, 0], dram_tokens(x, 0)).then_inc(x_loaded, 16)
            sp.dma_start(cst[:], consts).then_inc(consts_loaded, 16)
            for n, w in (("q", wq), ("k", wk), ("v", wv)):
                sp.dma_start(W[n][:], w.rearrange("(c p) n -> p c n", p=P)).then_inc(w_loaded[n], 16)
            sp.dma_start(W["o"][:], wo.rearrange("(c p) n -> p c n", p=P)).then_inc(w_loaded["o"], 16)
            for dst, src in ((table[:, TG:TG + DS * GRID], bases.rearrange("n j g -> n (j g)")),
                             (table[:, TS:TS + DS * GRID], slopes.rearrange("n j g -> n (j g)")),
                             (table[:, TGA:TGA + 1], oscale.unsqueeze(1)),
                             (table[:, TBE:TBE + DS], gamma.rearrange("(n j) -> n j", j=DS)),
                             (table[:, TBT:TBT + DS], beta.rearrange("(n j) -> n j", j=DS))):
                sp.dma_start(dst, src).then_inc(table_loaded, 16)
            with sp.Fori(1, NB) as b:
                sp.wait_ge(x_loaded, 16 * b)
                sp.dma_start(xs_all[:, b], x[b].rearrange("(p t) f -> p t f", t=T)).then_inc(x_loaded, 16)
            with sp.Fori(0, NB) as b:
                sp.wait_ge(res_ready, b + 1)
                sp.dma_start(out[b].rearrange("(p t) f -> p t f", t=T), res[:, b]).then_inc(stored, 16)
            sp.wait_ge(stored, 16 * NB)

        @block.gpsimd
        def _(pool):
            chain = Chain(pool, pool_chain)

            def rstd(dst, var, tmp, eps=EPS):
                chain(pool.tensor_scalar(tmp, var, eps, None, ALU.add))
                return pool.tensor_tensor(dst, tmp, half[:, 0:T], ALU.pow)

            def x_scale(b):
                pool.wait_ge(x_stats, b + 1)
                rstd(rst[:, 0, :], mv[:, 0, :, 1], tmpv[:, 0, :]).then_inc(x_rstd, 1)

            def post(b, n):
                r = slice(T * b, T * b + T) if isinstance(b, int) else bass.ds(T * b, T)
                pool.wait_ge(a_stats, n)
                rstd(rst[:, 1, :], mv[:, 1, :, 1], tmpv[:, 1, :]).then_inc(a_rstd, 1)
                pool.wait_ge(attn_normed, n)
                pool.tensor_tensor(x1[:, b], attn_n[:], xs_all[:, b], ALU.add).then_inc(x1_ready, 1)
                pool.wait_ge(x1_stats, n)
                chain(rstd(r1[:, r], mv1[:, r, 1], tmpv[:, 2, :]))
                chain(pool.tensor_tensor(tmpv[:, 0, :], r1[:, r], r1[:, r], ALU.mult))
                chain(pool.tensor_tensor(vy[:, r], tmpv[:, 0, :], mv1[:, r, 1], ALU.mult))
                rstd(r2[:, r], vy[:, r], tmpv[:, 2, :]).then_inc(x1_rstd, 1)
                pool.wait_ge(onehot_ready, n)
                pool.tensor_tensor(pick[:].rearrange("p t (n j) -> p (t n) j", j=DS),
                                   y[:, b].rearrange("p t (n j) -> p (t n) j", j=DS),
                                   onehot[:, r, :].rearrange("p t n -> p (t n)").unsqueeze(2)
                                   .broadcast_to([P, T * NTILE, DS]), ALU.mult).then_inc(picked, 1)

            def body(ph):
                if not ph.last:
                    x_scale(ph.b + 1)
                if not ph.first:
                    post(ph.b - 1, ph.b)

            pool.memset(V[:, :, :, DH:DH + 1], 1.0).then_inc(ones_set, 1)
            chain(pool.memset(half[:], -0.5))
            x_scale(0)
            run(pool, body)
            post(NB - 1, NB)
            pool.wait_ge(var3_ready, 1)
            pool.tensor_tensor(r3[:], s2[:], half[:], ALU.pow).then_inc(r3_ready, 1)
            pool.wait_ge(dr_ready, 1)
            with pool.Fori(0, NB) as b:
                spread(pool, put[:, b, 0, :], T * b).then_inc(put_ready, 1)

        @block.scalar
        def _(act):
            with nc.allow_non_contiguous_dma(reason="256 biases, one to a partition"):
                for i, v in enumerate((bq, bk)):
                    act.dma_start(bqk[:, i, :], v.rearrange("(c p) -> p c", p=P)).then_inc(bqk_loaded, 16)
                for i, v in enumerate((gamma, beta)):
                    act.dma_start(gbT[:, i, :], v.rearrange("(c p) -> p c", p=P)).then_inc(gbT_loaded, 16)
            act.dma_start(slp[:], slopes.rearrange("(c n) j g -> (n j) c g", c=KC)).then_inc(slp_loaded, 16)
            act.dma_start(bv_rows[:], bv.unsqueeze(0).broadcast_to([P, F])).then_inc(bv_loaded, 16)
            act.dma_start(bo_rows[:], bo.unsqueeze(0).broadcast_to([P, F])).then_inc(bo_loaded, 16)

            def evacuate(ph, name, emit, done):
                bank, n = ph.fill(name)
                act.wait_ge(filled[bank], n)
                emit(psX[bank]).then_inc(done, 1)

            def project(ph, m, name):
                if name == "q":
                    evacuate(ph, f"q{m}", lambda ps: act.activation(
                        qT[:, m, :], ps[:], ACT.Identity, bias=bqh[:, m:m + 1], scale=0.5), qk_ready)
                else:
                    evacuate(ph, f"k{m}", lambda ps: act.activation(
                        kT[:, m, :], ps[:], ACT.Identity, bias=bqk[:, 1, m:m + 1], scale=1.0), qk_ready)

            def xn_turned(ph, c):
                evacuate(ph, f"xt{c}", lambda ps: act.copy(xnT[:, c, :], ps[:]), xnT_ready)

            def feats_turned(ph, c):
                evacuate(ph, f"ft{c}", lambda ps: act.copy(featsT[:, c, :], ps[:]), featsT_ready)

            def scale_y(b, n):
                act.wait_ge(y_ready, n)
                for t in range(T):
                    col = T * b + t
                    ins = act.activation(yn[:, t, :], y[:, b, t, :], ACT.Copy,
                                         scale=r2[:, col:col + 1] if isinstance(b, int) else r2[:, bass.ds(col, 1)])
                ins.then_inc(yn_ready, 1)

            def signs(ph, c):
                evacuate(ph, f"yt{c}", lambda ps: act.activation(
                    signT[:, c, :], ps[:], ACT.Sign, bias=gbT[:, 1, c:c + 1], scale=gbT[:, 0, c:c + 1]), sign_ready)

            def onehot_turned(ph, b):
                evacuate(ph, "oht", lambda ps: act.copy(onehotT[:, b, :], ps[0:NTILE, :]), onehotT_ready)

            def rows_gathered(ph, b, i):
                col = T * b + 2 * i
                dst = G[:, col:col + 2, :] if isinstance(b, int) else G[:, bass.ds(col, 2), :]
                evacuate(ph, f"ga{i}", lambda ps: act.copy(
                    dst, ps[:, 0:2 * TW].rearrange("p (t w) -> p t w", t=2)), gathered)

            def exp(g, u):
                act.wait_ge(max_ready, g + 1)
                if not (isinstance(g, int) and g < 4):
                    act.wait_ge(turned, g - 3)
                act.activation(probs[:, u % 4, :], psS[u % 2][:], ACT.Exp, bias=nmax[:, u:u + 1],
                               scale=1.0).then_inc(probs_ready, 1)

            def copy_turned(g, u):
                act.wait_ge(turned, g + 1)
                if not (isinstance(g, int) and g < 4):
                    act.wait_ge(pv_done, g - 3)
                act.copy(probsT[:, u % 4, :], psT[u % 2][:]).then_inc(turned_act, 1)

            def body(ph):
                b = ph.b
                for u in range(HT):
                    g = HT * b + u
                    if u % 2 == 0 and not (ph.first and u < 2):
                        copy_turned(g - 2, (u - 2) % HT)
                    exp(g, u)
                    if u == 3:
                        project(ph, 1, "q")
                    if u == 4:
                        project(ph, 1, "k")
                    if u == 4 and not ph.first:
                        feats_turned(ph, 0)
                        feats_turned(ph, 1)
                    if u == 8 and not ph.last:
                        xn_turned(ph, 0)
                    if u == 9 and not ph.last:
                        xn_turned(ph, 1)
                    if u == 10 and not ph.last:
                        project(ph, 0, "q")
                    if u == 10 and not ph.first:
                        scale_y(b - 1, b)
                    if u == 11 and not ph.first:
                        signs(ph, 0)
                        signs(ph, 1)
                    if u == 12 and not ph.last:
                        project(ph, 0, "k")
                    if u == 14 and not ph.first:
                        onehot_turned(ph, b - 1)
                    if u == 15 and not ph.first:
                        rows_gathered(ph, b - 1, 0)
                        rows_gathered(ph, b - 1, 1)

            act.wait_ge(bqk_loaded, 32)
            act.mul(bqh[:], bqk[:, 0, :], 0.5).then_inc(bqh_ready, 1)
            act.wait_ge(ssum_ready, 1)
            act.activation(ssgn[:], ssum[:], ACT.Sign).then_inc(ssgn_ready, 1)
            act.wait_ge(bqh_ready, 1)
            pro = Phase(0, "prologue")
            xn_turned(pro, 0)
            xn_turned(pro, 1)
            project(pro, 0, "q")
            project(pro, 0, "k")
            act.wait_ge(gbT_loaded, 32)
            run(act, body)
            copy_turned(HT * NB - 2, HT - 2)
            tail = Phase(NB, "tail")
            feats_turned(tail, 0)
            feats_turned(tail, 1)
            scale_y(NB - 1, NB)
            signs(tail, 0)
            signs(tail, 1)
            onehot_turned(tail, NB - 1)
            rows_gathered(tail, NB - 1, 0)
            rows_gathered(tail, NB - 1, 1)

        @block.vector
        def _(dve):
            chain = Chain(dve, dve_chain)

            def stats(src, group, mean_var, done):
                for t in range(T):
                    ins = dve.bn_stats(st6[:, group, t, :], src(t))
                chain(ins)
                for t in range(T):
                    ins = dve.bn_aggr(mean_var(t), st6[:, group, t, :])
                ins.then_inc(done, 1)

            def x_norm_stats(b):
                dve.wait_ge(x_loaded, 16 * (b + 1))
                stats(lambda t: xs_all[:, b, t, :], 0, lambda t: mv[:, 0, t, :], x_stats)

            def x_norm(b):
                dve.wait_ge(x_rstd, b + 1)
                for t in range(T):
                    ins = dve.tensor_scalar(xn[:, t, :], xs_all[:, b, t, :], mv[:, 0, t, 0:1],
                                            rst[:, 0, t:t + 1], ALU.subtract, ALU.mult)
                ins.then_inc(xn_ready, 1)

            def values(ph, m):
                bank, n = ph.fill(f"v{m}")
                dve.wait_ge(filled[bank], n)
                for t in range(T):
                    ins = dve.tensor_tensor(
                        V[:, t, 2 * m:2 * m + 2, 0:DH],
                        psX[bank][:, t * P:t * P + P].rearrange("p (h d) -> p h d", h=2),
                        bv_rows[:, m * P:m * P + P].rearrange("p (h d) -> p h d", h=2), ALU.add)
                ins.then_inc(v_ready, 1)

            def row_max(g, u):
                dve.wait_ge(scores_ready, g + 1)
                dve.tensor_reduce(nmax[:, u:u + 1], psS[u % 2][:], AX.X, ALU.max,
                                  negate=True).then_inc(max_ready, 1)

            def copy_turned(g, u):
                dve.wait_ge(turned, g + 1)
                if not (isinstance(g, int) and g < 4):
                    dve.wait_ge(pv_done, g - 3)
                dve.tensor_copy(probsT[:, u % 4, :], psT[u % 2][:]).then_inc(turned_dve, 1)

            def head_norm(g, h):
                dve.wait_ge(pv_done, g + 1)
                o = psV[h % 2][:, 0:T * (DH + 1)].rearrange("p (t d) -> p t d", t=T)
                chain(dve.reciprocal(rsum[:, h, :], o[:, :, DH]))
                dve.tensor_tensor(feats[:, :, h * DH:(h + 1) * DH], o[:, :, 0:DH],
                                  rsum[:, h, :].unsqueeze(2).broadcast_to([P, T, DH]),
                                  ALU.mult).then_inc(feats_ready, 1)

            def attn_bias(ph):
                for i in range(2):
                    bank, n = ph.fill(f"o{i}")
                    dve.wait_ge(filled[bank], n)
                    ins = dve.tensor_tensor(attn[:, 2 * i:2 * i + 2, :],
                                            psX[bank][:].rearrange("p (t f) -> p t f", t=2),
                                            bo_rows[:].unsqueeze(1).broadcast_to([P, 2, F]), ALU.add)
                    ins.then_inc(o_copied, 1)
                dve.wait_ge(o_copied, 2 * ph.b)
                stats(lambda t: attn[:, t, :], 1, lambda t: mv[:, 1, t, :], a_stats)

            def attn_norm(n):
                dve.wait_ge(a_rstd, n)
                for t in range(T):
                    ins = dve.tensor_scalar(attn_n[:, t, :], attn[:, t, :], mv[:, 1, t, 0:1],
                                            rst[:, 1, t:t + 1], ALU.subtract, ALU.mult)
                ins.then_inc(attn_normed, 1)

            def one(ap, col):
                return ap[:, col:col + 1] if isinstance(col, int) else ap[:, bass.ds(col, 1)]

            def rows(b):
                return slice(T * b, T * b + T) if isinstance(b, int) else bass.ds(T * b, T)

            def x1_stats_of(b, n):
                dve.wait_ge(x1_ready, n)
                stats(lambda t: x1[:, b, t, :], 2, lambda t: one(mv1, T * b + t)
                      .rearrange("p o c -> p (o c)"), x1_stats)

            def y_of(b, n):
                dve.wait_ge(x1_rstd, n)
                for t in range(T):
                    ins = dve.tensor_scalar(y[:, b, t, :], x1[:, b, t, :],
                                            one(mv1, T * b + t)[:, 0, 0:1],
                                            one(r1, T * b + t), ALU.subtract, ALU.mult)
                ins.then_inc(y_ready, 1)

            def choose(ph, b):
                bank, n = ph.fill("key")
                dve.wait_ge(filled[bank], n)
                ins = dve.tensor_tensor(keys[:], psX[bank][:, 0:T * NTILE].rearrange("p (t n) -> p t n", t=T),
                                        tie.unsqueeze(1).broadcast_to([P, T, NTILE]), ALU.add)
                ins.then_inc(key_copied, 1)
                dve.wait_ge(key_copied, b + 1)
                chain(dve.tensor_reduce(kmax[:], keys[:], AX.X, ALU.max))
                ins = dve.tensor_tensor(onehot[:, rows(b), :], keys[:],
                                        kmax[:].unsqueeze(2).broadcast_to([P, T, NTILE]), ALU.is_equal)
                ins.then_inc(onehot_ready, 1)
                dve.wait_ge(onehot_ready, b + 1)
                dve.tensor_scalar(far[:], onehot[:, rows(b), :], -2 * FAR, FAR, ALU.mult, ALU.add)

            def extremes(b, n):
                r = rows(b)
                dve.wait_ge(picked, n)
                chain(dve.tensor_reduce(ysl[:, r, :], pick[:].rearrange("p t (n j) -> p t j n", j=DS),
                                        AX.X, ALU.add))
                chain(dve.tensor_tensor(xsl[:, r, :], ysl[:, r, :],
                                        r2[:, r].unsqueeze(2).broadcast_to([P, T, DS]), ALU.mult))
                dve.wait_ge(gathered, 2 * n)
                chain(dve.tensor_tensor(xsl[:, r, :], xsl[:, r, :], G[:, r, TBE:TBE + DS], ALU.mult))
                chain(dve.tensor_tensor(xsl[:, r, :], xsl[:, r, :], G[:, r, TBT:TBT + DS], ALU.add))
                dve.tensor_reduce(tmn[:, 0, :], xsl[:, r, :], AX.X, ALU.min)
                chain(dve.tensor_reduce(tmn[:, 1, :], xsl[:, r, :], AX.X, ALU.max, negate=True))
                for t in range(T):
                    for e in range(2):
                        ins = dve.scalar_tensor_tensor(out=acc[:, e, :], in0=far[:, t, :],
                                                       scalar=tmn[:, e, t:t + 1], in1=acc[:, e, :],
                                                       op0=ALU.max, op1=ALU.min)
                    chain(ins)

            def body(ph):
                b = ph.b
                for u in range(HT):
                    g = HT * b + u
                    row_max(g, u)
                    if u % 2 == 1 and not (ph.first and u < 2):
                        copy_turned(g - 2, (u - 2) % HT)
                    if u % 4 == 3 and not (ph.first and u == 3):
                        head_norm(g - 4, (u // 4 - 1) % H)
                    if u == 4 and not ph.last:
                        x_norm_stats(b + 1)
                    if u == 5:
                        values(ph, 1)
                    if u == 6 and not ph.last:
                        x_norm(b + 1)
                    if u == 6 and not ph.first:
                        attn_bias(ph)
                    if u == 7 and not ph.first:
                        attn_norm(b)
                    if u == 9 and not ph.first:
                        x1_stats_of(b - 1, b)
                    if u == 10 and not ph.first:
                        y_of(b - 1, b)
                    if u == 13 and not ph.last:
                        values(ph, 0)
                    if u == 13 and not ph.first:
                        choose(ph, b - 1)
                    if u == 15 and not ph.first:
                        extremes(b - 1, b)

            pro = Phase(0, "prologue")
            dve.memset(acc[:], FAR)
            x_norm_stats(0)
            x_norm(0)
            dve.wait_ge(slp_loaded, 16)
            dve.tensor_reduce(ssum[:], slp[:], AX.X, ALU.add).then_inc(ssum_ready, 1)
            dve.wait_ge(consts_loaded, 16)
            dve.wait_ge(ssgn_ready, 1)
            for c in range(KC):
                ins = dve.tensor_scalar(route[:, c, :], rmask[:, c, :], ssgn[:, c:c + 1], None, ALU.mult)
            ins.then_inc(route_ready, 1)
            dve.wait_ge(bv_loaded, 16)
            values(pro, 0)
            dve.wait_ge(bo_loaded, 16)
            run(dve, body)
            tail = Phase(NB, "tail")
            copy_turned(HT * NB - 1, HT - 1)
            head_norm(HT * NB - 1, H - 1)
            attn_bias(tail)
            attn_norm(NB)
            x1_stats_of(NB - 1, NB)
            y_of(NB - 1, NB)
            choose(tail, NB - 1)
            extremes(NB - 1, NB)
            dve.engine_nop().then_inc(acc_ready, 1)

            dve.wait_ge(accT_ready, 1)
            dve.tensor_reduce(tmm[:], psT[0][0:NTILE, 0:2 * P].rearrange("p (e n) -> p e n", e=2),
                              AX.X, ALU.min).then_inc(tmm_ready, 1)
            dve.wait_ge(lohi_filled, 1)
            chain(dve.tensor_copy(lohi[:], psT[1][:, 0:2 * NT].rearrange("p (n e) -> p n e", e=2)))
            chain(dve.scalar_tensor_tensor(out=rden[:], in0=lohi[:, :, 1], scalar=-1.0,
                                           in1=lohi[:, :, 0], op0=ALU.mult, op1=ALU.subtract))
            chain(dve.tensor_scalar(rden[:], rden[:], 1e-8, None, ALU.add))
            chain(dve.reciprocal(rden[:], rden[:]))
            chain(dve.tensor_tensor(u16[:], xsl[:], lohi[:, :, 0].unsqueeze(2).broadcast_to([P, NT, DS]),
                                    ALU.subtract))
            chain(dve.tensor_tensor(u16[:], u16[:], rden[:].unsqueeze(2).broadcast_to([P, NT, DS]), ALU.mult))
            chain(dve.tensor_scalar(u16[:], u16[:], 0.0, 1.0 - 1e-6, ALU.max, ALU.min))
            chain(dve.tensor_scalar(u16[:], u16[:], float(GRID), None, ALU.mult))
            chain(dve.tensor_scalar(gi[:], u16[:], MAGIC, MAGIC, ALU.add, ALU.subtract))
            chain(dve.tensor_tensor(over[:], gi[:], u16[:], ALU.is_gt))
            chain(dve.tensor_tensor(gi[:], gi[:], over[:], ALU.subtract))
            dve.tensor_tensor(xloc[:], u16[:], gi[:], ALU.subtract)
            chain(dve.tensor_tensor(piece[:], gi[:].rearrange("p n j -> p (n j)").unsqueeze(2)
                                    .broadcast_to([P, NT * DS, GRID]),
                                    steps16.unsqueeze(1).broadcast_to([P, NT * DS, GRID]), ALU.is_equal))
            pc = piece[:].rearrange("p (n j) g -> p n (j g)", j=DS)
            for e in range(2):
                ins = dve.tensor_tensor(hit[:, :, e * DS:(e + 1) * DS, :].rearrange("p n j g -> p n (j g)"),
                                        G[:, :, e * DS * GRID:(e + 1) * DS * GRID], pc, ALU.mult)
            chain(ins)
            chain(dve.tensor_reduce(coef[:], hit[:], AX.X, ALU.add))
            chain(dve.tensor_tensor(delta[:], coef[:, :, DS:2 * DS], xloc[:], ALU.mult))
            chain(dve.tensor_tensor(delta[:], delta[:], coef[:, :, 0:DS], ALU.add))
            chain(dve.tensor_tensor(delta[:], delta[:], G[:, :, TGA:TGA + 1].broadcast_to([P, NT, DS]), ALU.mult))
            dve.tensor_reduce(s1[:], delta[:], AX.X, ALU.add)
            chain(dve.scalar_tensor_tensor(out=sq[:], in0=ysl[:], scalar=2.0, in1=delta[:],
                                           op0=ALU.mult, op1=ALU.add))
            chain(dve.tensor_tensor(sq[:], sq[:], delta[:], ALU.mult))
            chain(dve.tensor_reduce(s2[:], sq[:], AX.X, ALU.add))
            chain(dve.tensor_scalar(s1[:], s1[:], 1.0 / F, None, ALU.mult))
            chain(dve.scalar_tensor_tensor(out=s2[:], in0=s2[:], scalar=1.0 / F, in1=vy[:],
                                           op0=ALU.mult, op1=ALU.add))
            chain(dve.tensor_tensor(mr3[:], s1[:], s1[:], ALU.mult))
            chain(dve.tensor_tensor(s2[:], s2[:], mr3[:], ALU.subtract))
            dve.tensor_scalar(s2[:], s2[:], EPS, None, ALU.add).then_inc(var3_ready, 1)
            dve.wait_ge(r3_ready, 1)
            chain(dve.scalar_tensor_tensor(out=mr3[:], in0=s1[:], scalar=-1.0, in1=r3[:],
                                           op0=ALU.mult, op1=ALU.mult))
            ins = dve.tensor_tensor(delta[:], delta[:], r3[:].unsqueeze(2).broadcast_to([P, NT, DS]), ALU.mult)
            ins.then_inc(dr_ready, 1)
            dve.wait_ge(dr_ready, 1)
            with dve.Fori(0, NB) as b:
                for t in range(1, T):
                    spread(dve, put[:, b, t, :], T * b + t)
                for t in range(T):
                    ins = dve.scalar_tensor_tensor(out=base[:, b, t, :], in0=y[:, b, t, :],
                                                   scalar=r3[:, bass.ds(T * b + t, 1)],
                                                   in1=x1[:, b, t, :], op0=ALU.mult, op1=ALU.add)
                ins.then_inc(base_ready, 1)
                dve.wait_ge(base_ready, b + 1)
                dve.wait_ge(put_ready, b + 1)
                for t in range(T):
                    ins = dve.scalar_tensor_tensor(out=res[:, b, t, :],
                                                   in0=put[:, b, t, :],
                                                   scalar=mr3[:, bass.ds(T * b + t, 1)],
                                                   in1=base[:, b, t, :], op0=ALU.add, op1=ALU.add)
                ins.then_inc(res_ready, 1)

        @block.tensor
        def _(pe):
            def fill(ph, name, emit):
                bank, n = ph.fill(name)
                for s, v in before(ph, name):
                    pe.wait_ge(s, v)
                emit(psX[bank]).then_inc(filled[bank], 1)

            def turn(src):
                def emit(ps):
                    for t in range(T):
                        ins = pe.transpose(ps[:, t * P:(t + 1) * P], src(t), ident)
                    return ins
                return emit

            def proj_qk(name, m):
                def emit(ps):
                    for c in range(KC):
                        ins = pe.matmul(ps[:], W[name][:, c, m * P:(m + 1) * P], xnT[:, c, :],
                                        start=(c == 0), stop=(c == KC - 1))
                    return ins
                return emit

            def proj_v(m):
                def emit(ps):
                    for t in range(T):
                        for c in range(KC):
                            ins = pe.matmul(ps[:, t * P:(t + 1) * P], xnT[:, c, t * P:(t + 1) * P],
                                            W["v"][:, c, m * P:(m + 1) * P],
                                            start=(c == 0), stop=(c == KC - 1))
                    return ins
                return emit

            def proj_o(i):
                def emit(ps):
                    for t in (2 * i, 2 * i + 1):
                        for c in range(KC):
                            ins = pe.matmul(ps[:, (t % 2) * F:(t % 2 + 1) * F], featsT[:, c, t * P:(t + 1) * P],
                                            W["o"][:, c, :], start=(c == 0), stop=(c == KC - 1))
                    return ins
                return emit

            def key_sums(ps):
                for t in range(T):
                    for c in range(KC):
                        ins = pe.matmul(ps[:, t * NTILE:(t + 1) * NTILE], signT[:, c, t * P:(t + 1) * P],
                                        route[:, c, :], start=(c == 0), stop=(c == KC - 1))
                return ins

            def shared(ph, name):
                b = ph.b
                nb = b + 1
                done = b
                if ph.kind == "prologue":
                    nb = 0
                if name in ("xt0", "xt1"):
                    pe.wait_ge(xn_ready, nb + 1)
                    c = int(name[2])
                    fill(ph, name, turn(lambda t: xn[:, t, c * P:(c + 1) * P]))
                elif name in ("q0", "k0", "q1", "k1"):
                    pe.wait_ge(xnT_ready, KC * ((nb if name[1] == "0" else b) + 1))
                    fill(ph, name, proj_qk(name[0], int(name[1])))
                elif name in ("v0", "v1"):
                    fill(ph, name, proj_v(int(name[1])))
                elif name in ("ft0", "ft1"):
                    pe.wait_ge(feats_ready, H * done)
                    c = int(name[2])
                    fill(ph, name, turn(lambda t: feats[:, t, c * P:(c + 1) * P]))
                elif name in ("o0", "o1"):
                    pe.wait_ge(featsT_ready, KC * done)
                    fill(ph, name, proj_o(int(name[1])))
                elif name in ("yt0", "yt1"):
                    pe.wait_ge(yn_ready, done)
                    c = int(name[2])
                    fill(ph, name, turn(lambda t: yn[:, t, c * P:(c + 1) * P]))
                elif name == "key":
                    pe.wait_ge(sign_ready, KC * done)
                    fill(ph, name, key_sums)
                elif name == "oht":
                    pe.wait_ge(onehot_ready, done)

                    def emit(ps):
                        for t in range(T):
                            ins = pe.transpose(ps[0:NTILE, t * P:(t + 1) * P], onehot[:, T * (b - 1) + t, :], ident)
                        return ins
                    fill(ph, name, emit)
                else:
                    pe.wait_ge(onehotT_ready, done)
                    i = int(name[2])

                    def emit(ps):
                        for t in (2 * i, 2 * i + 1):
                            ins = pe.matmul(ps[:, (t % 2) * TW:(t % 2 + 1) * TW], onehotT[:, b - 1, t * P:(t + 1) * P],
                                            table[:], start=True, stop=True)
                        return ins
                    fill(ph, name, emit)

            def scores(g, u, b):
                h, t = u // T, u % T
                if t == 0 and h % 2 == 0:
                    pe.wait_ge(qk_ready, 2 * (2 * b + h // 2 + 1))
                if not (isinstance(g, int) and g < 2):
                    pe.wait_ge(probs_ready, g - 1)
                r = DH * (h % 2)
                pe.matmul(psS[u % 2][:], qT[r:r + DH, h // 2, t * P:(t + 1) * P], kT[r:r + DH, h // 2, :],
                          start=True, stop=True).then_inc(scores_ready, 1)

            def copied(b, u):
                pe.wait_ge(turned_dve if u % 2 else turned_act, (HT // 2) * b + u // 2 + 1)

            def transposes(b, u):
                g = HT * b + u
                pe.wait_ge(probs_ready, g + 1)
                if not (isinstance(g, int) and g < 2):
                    copied(b if u >= 2 else b - 1, (u - 2) % HT)
                for k in range(T):
                    ins = pe.transpose(psT[u % 2][:, k * P:(k + 1) * P], probs[:, u % 4, k * P:(k + 1) * P], ident)
                ins.then_inc(turned, 1)

            def weighted(b, u):
                h, t = u // T, u % T
                copied(b, u)
                if t == 0 and h % 2 == 0:
                    pe.wait_ge(v_ready, 2 * b + h // 2 + 1)
                if t == 0 and not (isinstance(b, int) and b == 0 and h < 2):
                    pe.wait_ge(feats_ready, H * b + h - 1)
                for k in range(T):
                    ins = pe.matmul(psV[h % 2][:, t * (DH + 1):(t + 1) * (DH + 1)],
                                    probsT[:, u % 4, k * P:(k + 1) * P], V[:, k, h, :],
                                    start=(k == 0), stop=(k == T - 1))
                ins.then_inc(pv_done, 1)

            def body(ph):
                b = ph.b
                for u in range(HT):
                    scores(HT * b + u, u, b)
                    if not (ph.first and u < 2):
                        transposes(b if u >= 2 else b - 1, (u - 2) % HT)
                    if not (ph.first and u < 3):
                        weighted(b if u >= 3 else b - 1, (u - 3) % HT)
                    for name, _ in SLOTS.get(u, []):
                        if name in dict(ph.fills):
                            shared(ph, name)

            pe.wait_ge(consts_loaded, 16)
            pro = Phase(0, "prologue")
            for name, _ in PROLOGUE:
                if name[0] in "qkv":
                    pe.wait_ge(w_loaded[name[0]], 16)
                shared(pro, name)
            pe.wait_ge(w_loaded["o"], 16)
            pe.wait_ge(route_ready, 1)
            pe.wait_ge(table_loaded, 16 * 5)
            pe.wait_ge(ones_set, 1)
            run(pe, body)
            last = NB - 1
            transposes(last, HT - 2)
            weighted(last, HT - 3)
            transposes(last, HT - 1)
            weighted(last, HT - 2)
            weighted(last, HT - 1)
            tail = Phase(NB, "tail")
            for name, _ in TAIL:
                shared(tail, name)
            pe.wait_ge(acc_ready, 1)
            for e in range(2):
                ins = pe.transpose(psT[0][0:NTILE, e * P:(e + 1) * P], acc[:, e, :], ident)
            ins.then_inc(accT_ready, 1)
            pe.wait_ge(tmm_ready, 1)
            for n in range(NT):
                ins = pe.matmul(psT[1][:, 2 * n:2 * n + 2], onehotT[:, n // T, (n % T) * P:(n % T + 1) * P],
                                tmm[:], start=True, stop=True)
            ins.then_inc(lohi_filled, 1)


_INS = ["L0_attn_x", "L0_attn_Wq", "L0_attn_bq", "L0_attn_Wk", "L0_attn_bk", "L0_attn_Wv", "L0_attn_bv",
        "L0_attn_Wo", "L0_attn_bo", "L0_ffn_ln_gamma", "L0_ffn_ln_beta", "L0_ffn_spline_bases",
        "L0_ffn_spline_slopes", "L0_ffn_output_scale"]


def shape_constants(np):
    c = np.zeros((P, CW), np.float32)
    c[:, 0:P] = np.eye(P)
    feature = np.arange(KC)[None, :, None] * P + np.arange(P)[:, None, None]
    tile = np.arange(NTILE)[None, None, :]
    mask = (1024 * (feature // (F // NCL) == tile // (NTILE // NCL)) + 8 * (feature // DS == tile))
    c[:, P:P + KC * NTILE] = mask.reshape(P, KC * NTILE)
    n = np.arange(NTILE)
    c[:, P + KC * NTILE:P + KC * NTILE + NTILE] = 128 * (NCL - 1 - n // NCL) + (NCL - 1 - n % NCL)
    c[:, P + KC * NTILE + NTILE:] = np.arange(GRID)
    return c


def kernel(**inputs):
    import numpy as _np
    import concourse.bacc as _bacc
    from concourse.bass_utils import run_bass_kernel_spmd as _run

    nc = _bacc.Bacc("TRN2", target_bir_lowering=False, num_devices=1)
    arrays = {f"in_{n}": _np.ascontiguousarray(inputs[n]) for n in _INS}
    arrays["in_shape_constants"] = shape_constants(_np)
    args = [nc.dram_tensor(n, a.shape, mybir.dt.from_np(a.dtype), kind="ExternalInput").ap()
            for n, a in arrays.items()]
    args.append(nc.dram_tensor("out_dram", (NB, SEQ, F), F32, kind="ExternalOutput").ap())
    sandwich(nc, *args)
    r = _run(nc, [arrays], core_ids=[0])
    return r.results[0]["out_dram"]
```

```python
from contextlib import ExitStack

import concourse.bass as bass
from concourse import mybir

F32 = mybir.dt.float32
F32R = mybir.dt.float32r
BF16 = mybir.dt.bfloat16
ALU = mybir.AluOpType
ACT = mybir.ActivationFunctionType
AX = mybir.AxisListType

P = 128
NB, SEQ, F = 4, 512, 256
T = SEQ // P
NT = NB * T
KC = F // P
H, DH = 4, 64
UB = H * T
NU = NB * UB
NTILE, DS, GRID = 64, 4, 16
NCL = 8
EPS = 1e-5
FAR = 1e38
MAGIC = 1.5 * 2.0 ** 23
TW = 2 * DS * GRID + 1 + 2 * DS
TG, TS, TGA, TBE = 0, DS * GRID, 2 * DS * GRID, 2 * DS * GRID + 1
TBT = TBE + DS
CW = P + KC * NTILE + NTILE + GRID

GROUPS = [(n, 2) for n in range(0, NT - 2, 2)] + [(NT - 2, 1), (NT - 1, 1)]
GT = 2
CHUNKS = [(0, NT // 2), (NT // 2, NT // 2)]

TURN, WEIGH = 3, 4
NS = 3

PREP_PE = [("xt0", -12), ("xt1", -11), ("q0", -10), ("k0", -8), ("q1", -7), ("k1", -5), ("va", -4), ("vb", -3)]
FIRST_PREP_PE = [("xt0", -12), ("xt1", -11), ("q0", -10), ("k0", -9), ("q1", -8), ("k1", 0), ("va", 1), ("vb", 2)]
X_STATS, X_NORM = (-16, -15), (-14, -13)
POST_PE = [("ft", 1), ("o", 3), ("yt", 10), ("key", 12), ("oht", 14), ("ga", 15)]
NORM, O_COPY, ATTN_STATS, RESIDUAL, X1_STATS, YN, CHOOSE, PICKED, EXTREMES = 1, 4, 5, 7, 8, 10, 13, 15, 17
POST_ACT = {"ft": 2, "yt": 11, "oht": 15, "ga": 16}


def base_slot(j):
    n, size = GROUPS[j]
    return (n + size) * H - 1 + WEIGH


def prep_slots(b):
    return [(name, UB * b + at) for name, at in (FIRST_PREP_PE if b == 0 else PREP_PE)]


def all_fills():
    fills = [(at, name, b) for b in range(NB) for name, at in prep_slots(b)]
    fills += [(base_slot(j) + at, name, j) for j in range(len(GROUPS)) for name, at in POST_PE]
    return sorted(fills, key=lambda f: f[0])


FILLS = all_fills()
ORDER = {(name, i): at for at, (_, name, i) in enumerate(FILLS)}
LAST_SLOT = base_slot(len(GROUPS) - 1) + EXTREMES


def bank_of(name, i):
    return ORDER[name, i] % 2


def filled_count(name, i):
    return ORDER[name, i] // 2 + 1


def on_dve(g):
    return g % 4 == 3


def sandwich(nc, x, wq, bq, wk, bk, wv, bv, wo, bo, gamma, beta, bases, slopes, oscale, consts, out):
    with ExitStack() as ctx:
        def sb(name, shape, dt=F32):
            return ctx.enter_context(nc.sbuf_tensor(name, shape, dt))

        def sem(name):
            return ctx.enter_context(nc.semaphore(name))

        x_in = sb("x_in", [P, NT, F])
        x1 = sb("x1", [P, NT, F])
        xn = sb("xn", [P, T, F])
        xnT_hi, xnT_lo = sb("xnT_hi", [P, KC, SEQ], F32R), sb("xnT_lo", [P, KC, SEQ], F32R)
        W = {n: sb("w" + n, [P, KC, F]) for n in "qkvo"}
        W_hi = {n: sb(f"w{n}_hi", [P, KC, F], F32R) for n in "qkv"}
        W_lo = {n: sb(f"w{n}_lo", [P, KC, F], F32R) for n in "qkv"}
        bqk = sb("bqk", [P, 2, KC])
        bias_qk = sb("bias_qk", [P, 2, KC])
        bv_rows = sb("bv_rows", [P, F])
        bo_rows = sb("bo_rows", [P, F])
        gbT = sb("gbT", [P, 2, KC])
        cst = sb("cst", [P, CW])
        ident_b = sb("ident_b", [P, P], BF16)
        q_hi, q_lo = sb("q_hi", [P, 2, KC, SEQ], F32R), sb("q_lo", [P, 2, KC, SEQ], F32R)
        k_hi, k_lo = sb("k_hi", [P, 2, KC, SEQ], F32R), sb("k_lo", [P, 2, KC, SEQ], F32R)
        V = sb("V", [P, 2, T, H, DH + 1])
        probs = sb("probs", [P, 4, SEQ])
        probsT = sb("probsT", [P, 4, SEQ])
        nmax = sb("nmax", [P, 8])
        rsum = sb("rsum", [P, 2, H])
        feats = sb("feats", [P, GT, F])
        featsT = sb("featsT", [P, GT, KC, P])
        attn = sb("attn", [P, GT, F])
        yn = sb("yn", [P, GT, F])
        signT = sb("signT", [P, KC, GT * P], BF16)
        route = sb("route", [P, KC, NTILE], BF16)
        slp = sb("slp", [P, KC, GRID])
        ssum = sb("ssum", [P, KC])
        ssgn = sb("ssgn", [P, KC])
        keys = sb("keys", [P, GT, NTILE])
        kmax = sb("kmax", [P, GT])
        onehot = sb("onehot", [P, NT, NTILE], BF16)
        onehotT = sb("onehotT", [NTILE, NT, P], BF16)
        table = sb("table", [NTILE, TW])
        table_rest = sb("table_rest", [NTILE, TW])
        table_b = [sb(f"table_b{i}", [NTILE, TW], BF16) for i in range(3)]
        G = sb("G", [P, NT, TW])
        pick = sb("pick", [P, GT, F])
        far = sb("far", [P, 2, GT, NTILE])
        nsl = sb("nsl", [P, NT, DS])
        xsl = sb("xsl", [P, NT, DS])
        tmn = sb("tmn", [P, 2, GT])
        acc = sb("acc", [P, 2, NTILE])
        st6 = sb("st6", [P, T, 6])
        st6a = sb("st6a", [P, GT, 6])
        st61 = sb("st61", [P, GT, 6])
        mvx = sb("mvx", [P, T, 2])
        rx = sb("rx", [P, T])
        mva = sb("mva", [P, NT, 2])
        ra = sb("ra", [P, NT])
        mv1 = sb("mv1", [P, NT, 2])
        r12 = sb("r12", [P, NT])
        nb12 = sb("nb12", [P, NT])
        nm1 = sb("nm1", [P, NT])
        r1 = sb("r1", [P, NT])
        vy = sb("vy", [P, NT])
        sy = sb("sy", [P, NT])
        vt = [sb(f"vt{i}", [P, NT]) for i in range(5)]
        mhalf = sb("mhalf", [P, NT])
        phalf = sb("phalf", [P, NT])
        tmm = sb("tmm", [NTILE, 2])
        tmm_rest = sb("tmm_rest", [NTILE, 2])
        tmm_b = [sb(f"tmm_b{i}", [NTILE, 2], BF16) for i in range(3)]
        lohi = sb("lohi", [P, NT, 2])
        rden = sb("rden", [P, NT])
        u16 = sb("u16", [P, NT, DS])
        gi = sb("gi", [P, NT, DS])
        over = sb("over", [P, NT, DS])
        xloc = sb("xloc", [P, NT, DS])
        piece = sb("piece", [P, NT * DS // 2, GRID])
        hit = sb("hit", [P, NT // 2, 2 * DS, GRID])
        coef = sb("coef", [P, NT, 2 * DS])
        delta = sb("delta", [P, NT, DS])
        sq = sb("sq", [P, NT, DS])
        s1 = sb("s1", [P, NT])
        s2 = sb("s2", [P, NT])
        r3 = sb("r3", [P, NT])
        c1 = sb("c1", [P, NT])
        c0 = sb("c0", [P, NT])
        rows_b = sb("rows_b", [P, NT, F])
        put = sb("put", [P, NT, F])
        res = x_in

        psS = [ctx.enter_context(nc.psum_tensor(f"psS{i}", [P, SEQ], F32)) for i in range(NS)]
        psT = ctx.enter_context(nc.psum_tensor("psT", [P, SEQ], F32))
        psV = [ctx.enter_context(nc.psum_tensor(f"psV{i}", [P, SEQ], F32)) for i in range(2)]
        psX = [ctx.enter_context(nc.psum_tensor(f"psX{i}", [P, SEQ], F32)) for i in range(2)]

        ident = cst[:, 0:P]
        rmask = cst[:, P:P + KC * NTILE].rearrange("p (c n) -> p c n", c=KC)
        tie = cst[:, P + KC * NTILE:P + KC * NTILE + NTILE]
        steps16 = cst[:, P + KC * NTILE + NTILE:CW]

        x_loaded, consts_loaded, bv_loaded = sem("x_loaded"), sem("consts_loaded"), sem("bv_loaded")
        w_loaded = {n: sem("w_loaded_" + n) for n in "qkvo"}
        w_hi_ready = {n: sem(f"w{n}_hi_ready") for n in "qkv"}
        w_lo_ready = {n: sem(f"w{n}_lo_ready") for n in "qkv"}
        bqk_loaded, gbT_loaded, slp_loaded = sem("bqk_loaded"), sem("gbT_loaded"), sem("slp_loaded")
        bo_loaded, table_loaded, stored = sem("bo_loaded"), sem("table_loaded"), sem("stored")
        ones_set, ident_b_ready, table_ready = sem("ones_set"), sem("ident_b_ready"), sem("table_ready")
        bias_ready, ssum_ready, ssgn_ready, route_ready = (sem("bias_ready"), sem("ssum_ready"),
                                                           sem("ssgn_ready"), sem("route_ready"))
        x_stats, x_rstd, xn_ready = sem("x_stats"), sem("x_rstd"), sem("xn_ready")
        filled = [sem("filled0"), sem("filled1")]
        xnT_hi_ready, xnT_ready = sem("xnT_hi_ready"), sem("xnT_ready")
        qk_hi_ready, qk_ready, v_ready = sem("qk_hi_ready"), sem("qk_ready"), sem("v_ready")
        scores_ready, max_ready, probs_ready = sem("scores_ready"), sem("max_ready"), sem("probs_ready")
        turned, turned_act, turned_dve = sem("turned"), sem("turned_act"), sem("turned_dve")
        pv_done, feats_ready, featsT_ready = sem("pv_done"), sem("feats_ready"), sem("featsT_ready")
        x1_ready = sem("x1_ready")
        o_copied, a_stats, a_rstd, x1_stats, x1_scale = (sem("o_copied"), sem("a_stats"), sem("a_rstd"),
                                                         sem("x1_stats"), sem("x1_scale"))
        yn_ready, sign_ready, key_copied, onehot_ready = (sem("yn_ready"), sem("sign_ready"),
                                                          sem("key_copied"), sem("onehot_ready"))
        onehotT_ready, picked, gathered = sem("onehotT_ready"), sem("picked"), sem("gathered")
        nsl_ready = sem("nsl_ready")
        acc_ready, accT_ready, tmm_ready, lohi_filled = (sem("acc_ready"), sem("accT_ready"),
                                                         sem("tmm_ready"), sem("lohi_filled"))
        scales_ready, var3_ready, r3_ready, c_ready = (sem("scales_ready"), sem("var3_ready"),
                                                       sem("r3_ready"), sem("c_ready"))
        rows_ready, put_ready, put_dve, res_ready = (sem("rows_ready"), sem("put_ready"), sem("put_dve"),
                                                     sem("res_ready"))
        dve_chain, pool_chain = sem("dve_chain"), sem("pool_chain")

        def copied_out(name, i):
            return {"xt0": (xnT_ready, 2 * i + 1), "xt1": (xnT_ready, 2 * i + 2),
                    "q0": (qk_ready, 4 * i + 1), "k0": (qk_ready, 4 * i + 2),
                    "q1": (qk_ready, 4 * i + 3), "k1": (qk_ready, 4 * i + 4),
                    "va": (v_ready, 2 * i + 1), "vb": (v_ready, 2 * i + 2),
                    "ft": (featsT_ready, i + 1), "o": (o_copied, i + 1), "yt": (sign_ready, i + 1),
                    "key": (key_copied, i + 1), "oht": (onehotT_ready, i + 1), "ga": (gathered, i + 1)}[name]

        def run(attention, tasks, turned_weights=lambda s: None, before=()):
            tasks = sorted(tasks, key=lambda task: task[0])
            before = sorted(before, key=lambda task: task[0])
            for s in range(min(task[0] for task in [(0,), *tasks, *before]), max(LAST_SLOT, NU + WEIGH) + 1):
                for at, step, args in before:
                    if at == s:
                        step(*args)
                if s >= 0:
                    attention(s)
                for at, step, args in tasks:
                    if at == s:
                        step(*args)
                if s >= 0:
                    turned_weights(s)

        def prep(name, emit, later=1):
            return [(at + later, emit, (b,)) for b in range(NB) for n, at in prep_slots(b) if n == name]

        def post(at, emit):
            return [(base_slot(j) + at, emit, (j,)) for j in range(len(GROUPS))]

        class Chain:

            def __init__(self, eng, s):
                self.eng, self.s, self.n = eng, s, 0

            def __call__(self, ins):
                self.n += 1
                ins.then_inc(self.s, 1)
                self.eng.wait_ge(self.s, self.n)

        def spread(eng, n):
            return eng.tensor_tensor(put[:, n, :].rearrange("p (n j) -> p n j", j=DS),
                                     onehot[:, n, :].unsqueeze(2).broadcast_to([P, NTILE, DS]),
                                     delta[:, n:n + 1, :].broadcast_to([P, NTILE, DS]), ALU.mult)

        def by_pool(n):
            return n % 3 == 2

        block = ctx.enter_context(nc.Block())

        @block.sync
        def _(sp):
            def load_x(b):
                sp.dma_start(x_in[:, T * b:T * b + T], x[b].rearrange("(p t) f -> p t f", t=T)).then_inc(x_loaded, 16)

            load_x(0)
            for n, w in (("q", wq), ("k", wk), ("v", wv)):
                sp.dma_start(W[n][:], w.rearrange("(c p) n -> p c n", p=P)).then_inc(w_loaded[n], 16)
            sp.dma_start(bv_rows[:], bv.unsqueeze(0).broadcast_to([P, F])).then_inc(bv_loaded, 16)
            sp.dma_start(slp[:], slopes.rearrange("(c n) j g -> (n j) c g", c=KC)).then_inc(slp_loaded, 16)
            sp.dma_start(W["o"][:], wo.rearrange("(c p) n -> p c n", p=P)).then_inc(w_loaded["o"], 16)
            sp.dma_start(bo_rows[:], bo.unsqueeze(0).broadcast_to([P, F])).then_inc(bo_loaded, 16)
            with nc.allow_non_contiguous_dma(reason="256 factors, one to a partition"):
                for i, v in enumerate((gamma, beta)):
                    sp.dma_start(gbT[:, i, :], v.rearrange("(c p) -> p c", p=P)).then_inc(gbT_loaded, 16)
            for dst, src in ((table[:, TG:TG + DS * GRID], bases.rearrange("n j g -> n (j g)")),
                             (table[:, TS:TS + DS * GRID], slopes.rearrange("n j g -> n (j g)")),
                             (table[:, TGA:TGA + 1], oscale.unsqueeze(1)),
                             (table[:, TBE:TBE + DS], gamma.rearrange("(n j) -> n j", j=DS)),
                             (table[:, TBT:TBT + DS], beta.rearrange("(n j) -> n j", j=DS))):
                sp.dma_start(dst, src).then_inc(table_loaded, 16)
            for b in range(1, NB):
                sp.wait_ge(x_loaded, 16 * b)
                load_x(b)
            for b in range(NB):
                for i in range(2):
                    sp.wait_ge(res_ready, 2 * b + i + 1)
                    sp.dma_start(out[b].rearrange("(p t) f -> p t f", t=T)[:, 2 * i:2 * i + 2],
                                 res[:, T * b + 2 * i:T * b + 2 * i + 2]).then_inc(stored, 16)
            sp.wait_ge(stored, 16 * 2 * NB)

        @block.gpsimd
        def _(pool):
            chain = Chain(pool, pool_chain)

            def x_scale(b):
                pool.wait_ge(x_stats, b + 1)
                chain(pool.tensor_scalar(vt[0][:, 0:T], mvx[:, :, 1], EPS, None, ALU.add))
                pool.tensor_tensor(rx[:], vt[0][:, 0:T], mhalf[:, 0:T], ALU.pow).then_inc(x_rstd, 1)

            def attn_scale(j):
                n, size = GROUPS[j]
                r = slice(n, n + size)
                pool.wait_ge(a_stats, j + 1)
                chain(pool.tensor_scalar(vt[1][:, r], mva[:, r, 1], EPS, None, ALU.add))
                pool.tensor_tensor(ra[:, r], vt[1][:, r], mhalf[:, r], ALU.pow).then_inc(a_rstd, 1)

            def yn_scale(j):
                n, size = GROUPS[j]
                r = slice(n, n + size)
                pool.wait_ge(x1_stats, j + 1)
                chain(pool.tensor_scalar(vt[2][:, r], mv1[:, r, 1], 1.0 + EPS, EPS * EPS, ALU.mult, ALU.add))
                chain(pool.tensor_tensor(r12[:, r], vt[2][:, r], mhalf[:, r], ALU.pow))
                chain(pool.tensor_scalar(nm1[:, r], mv1[:, r, 0], -1.0, None, ALU.mult))
                pool.tensor_tensor(nb12[:, r], nm1[:, r], r12[:, r], ALU.mult).then_inc(x1_scale, 1)

            def later_scales(j):
                n, size = GROUPS[j]
                r = slice(n, n + size)
                chain(pool.tensor_scalar(vt[3][:, r], mv1[:, r, 1], EPS, None, ALU.add))
                chain(pool.tensor_tensor(r1[:, r], vt[3][:, r], mhalf[:, r], ALU.pow))
                chain(pool.tensor_tensor(vt[4][:, r], r1[:, r], r1[:, r], ALU.mult))
                chain(pool.tensor_tensor(vy[:, r], vt[4][:, r], mv1[:, r, 1], ALU.mult))
                chain(pool.tensor_scalar(vt[3][:, r], vy[:, r], EPS, None, ALU.add))
                pool.tensor_tensor(sy[:, r], vt[3][:, r], phalf[:, r], ALU.pow).then_inc(scales_ready, 1)

            def pick_features(j):
                n, size = GROUPS[j]
                pool.wait_ge(onehot_ready, j + 1)
                for i in range(size):
                    ins = pool.tensor_tensor(pick[:, i, :].rearrange("p (n j) -> p n j", j=DS),
                                             yn[:, i, :].rearrange("p (n j) -> p n j", j=DS),
                                             onehot[:, n + i, :].unsqueeze(2).broadcast_to([P, NTILE, DS]),
                                             ALU.mult)
                ins.then_inc(picked, 1)

            pool.memset(V[:, :, :, :, DH:DH + 1], 1.0).then_inc(ones_set, 1)
            pool.memset(phalf[:], 0.5)
            chain(pool.memset(mhalf[:], -0.5))

            def split_table(_):
                pool.wait_ge(table_loaded, 16 * 5)
                chain(pool.tensor_copy(table_b[0][:], table[:]))
                chain(pool.tensor_tensor(table_rest[:], table[:], table_b[0][:], ALU.subtract))
                chain(pool.tensor_copy(table_b[1][:], table_rest[:]))
                pool.tensor_tensor(table_b[2][:], table_rest[:], table_b[1][:],
                                   ALU.subtract).then_inc(table_ready, 1)

            run(lambda s: None,
                [(UB * b + X_STATS[1], x_scale, (b,)) for b in range(NB)] + [(0, split_table, (0,))]
                + post(ATTN_STATS, attn_scale) + post(X1_STATS, yn_scale) + post(X1_STATS, later_scales)
                + post(CHOOSE, pick_features))
            for k, (n0, size) in enumerate(CHUNKS):
                r = slice(n0, n0 + size)
                pool.wait_ge(var3_ready, k + 1)
                pool.tensor_tensor(r3[:, r], s2[:, r], mhalf[:, r], ALU.pow).then_inc(r3_ready, 1)
            for k, (n0, size) in enumerate(CHUNKS):
                pool.wait_ge(c_ready, k + 1)
                for n in range(n0, n0 + size):
                    if by_pool(n):
                        spread(pool, n).then_inc(put_ready, 1)

        @block.scalar
        def _(act):
            def await_fill(name, i):
                act.wait_ge(filled[bank_of(name, i)], filled_count(name, i))
                return psX[bank_of(name, i)]

            def xn_turned(c):
                def step(b):
                    ps = await_fill(f"xt{c}", b)
                    act.copy(xnT_hi[:, c, :], ps[:]).then_inc(xnT_hi_ready, 1)
                return step

            def projected(name, m):
                def step(b):
                    ps = await_fill(f"{name}{m}", b)
                    i, hi = (0, q_hi) if name == "q" else (1, k_hi)
                    act.activation(hi[:, b % 2, m, :], ps[:], ACT.Identity, bias=bias_qk[:, i, m:m + 1],
                                   scale=1.0).then_inc(qk_hi_ready, 1)
                return step

            def feats_turned(j):
                size = GROUPS[j][1]
                ps = await_fill("ft", j)
                act.copy(featsT[:, 0:size].rearrange("p t c q -> p (t c q)"),
                         ps[:, 0:size * F]).then_inc(featsT_ready, 1)

            def normalize_y(j):
                n, size = GROUPS[j]
                act.wait_ge(x1_scale, j + 1)
                if j >= 1:
                    act.wait_ge(picked, j)
                for i in range(size):
                    ins = act.activation(yn[:, i, :], x1[:, n + i, :], ACT.Identity,
                                         bias=nb12[:, n + i:n + i + 1], scale=r12[:, n + i:n + i + 1])
                ins.then_inc(yn_ready, 1)

            def signs(j):
                size = GROUPS[j][1]
                ps = await_fill("yt", j)
                for c in range(KC):
                    ins = act.activation(signT[:, c, 0:size * P], ps[:, c * GT * P:c * GT * P + size * P],
                                         ACT.Sign, bias=gbT[:, 1, c:c + 1], scale=gbT[:, 0, c:c + 1])
                ins.then_inc(sign_ready, 1)

            def onehot_turned(j):
                n, size = GROUPS[j]
                ps = await_fill("oht", j)
                act.copy(onehotT[:, n:n + size, :].rearrange("q n p -> q (n p)"),
                         ps[0:NTILE, :].bitcast(BF16)[:, 0:size * P]).then_inc(onehotT_ready, 1)

            def rows_gathered(j):
                n, size = GROUPS[j]
                ps = await_fill("ga", j)
                act.copy(G[:, n:n + size, :].rearrange("p n w -> p (n w)"),
                         ps[:, 0:size * TW]).then_inc(gathered, 1)

            def exp(g):
                act.wait_ge(max_ready, g + 1)
                if g >= 4:
                    act.wait_ge(turned, g - 3)
                act.activation(probs[:, g % 4, :], psS[g % NS][:], ACT.Exp, bias=nmax[:, g % 8:g % 8 + 1],
                               scale=1.0).then_inc(probs_ready, 1)

            def copy_turned(g):
                act.wait_ge(turned, g + 1)
                if g >= 4:
                    act.wait_ge(pv_done, g - 3)
                act.copy(probsT[:, g % 4, :], psT[:]).then_inc(turned_act, 1)

            def attention(s):
                if s < NU:
                    exp(s)

            def turned_weights(s):
                if 0 <= s - TURN < NU and not on_dve(s - TURN):
                    copy_turned(s - TURN)

            act.dma_start(cst[:], consts).then_inc(consts_loaded, 16)
            with nc.allow_non_contiguous_dma(reason="256 biases, one to a partition"):
                for i, v in enumerate((bq, bk)):
                    act.dma_start(bqk[:, i, :], v.rearrange("(c p) -> p c", p=P)).then_inc(bqk_loaded, 16)
            act.wait_ge(bqk_loaded, 32)
            act.mul(bias_qk[:, 0, :], bqk[:, 0, :], 0.5)
            act.mul(bias_qk[:, 1, :], bqk[:, 1, :], 1.0).then_inc(bias_ready, 1)
            for n, f in (("q", 0.5), ("k", 1.0), ("v", 1.0)):
                act.wait_ge(w_loaded[n], 16)
                act.mul(W_hi[n][:], W[n][:], f).then_inc(w_hi_ready[n], 1)
            act.wait_ge(bias_ready, 1)

            def slope_signs(_):
                act.wait_ge(ssum_ready, 1)
                act.activation(ssgn[:], ssum[:], ACT.Sign).then_inc(ssgn_ready, 1)
                act.wait_ge(gbT_loaded, 32)

            tasks = post(POST_ACT["ft"], feats_turned) + post(YN, normalize_y) + post(POST_ACT["yt"], signs)
            tasks += post(POST_ACT["oht"], onehot_turned) + post(POST_ACT["ga"], rows_gathered)
            tasks += prep("xt0", xn_turned(0)) + prep("xt1", xn_turned(1))
            for m in range(KC):
                tasks += prep(f"q{m}", projected("q", m)) + prep(f"k{m}", projected("k", m))
            run(attention, [(1, slope_signs, (0,))], turned_weights, tasks)
            for k, (n0, size) in enumerate(CHUNKS):
                act.wait_ge(c_ready, k + 1)
                for n in range(n0, n0 + size):
                    act.activation(rows_b[:, n, :], x1[:, n, :], ACT.Identity, bias=c0[:, n:n + 1],
                                   scale=c1[:, n:n + 1]).then_inc(rows_ready, 1)

        @block.vector
        def _(dve):
            chain = Chain(dve, dve_chain)

            def await_fill(name, i):
                dve.wait_ge(filled[bank_of(name, i)], filled_count(name, i))
                return psX[bank_of(name, i)]

            def aggregate(mean_var, six, count, done):
                for t in range(count):
                    ins = dve.bn_aggr(mean_var(t), six[:, t, :])
                ins.then_inc(done, 1)

            def x_statistics(b, i):
                if i == 0:
                    dve.wait_ge(x_loaded, 16 * (b + 1))
                for t in (2 * i, 2 * i + 1):
                    ins = dve.bn_stats(st6[:, t, :], x_in[:, T * b + t, :])
                if i == 1:
                    chain(ins)
                    aggregate(lambda t: mvx[:, t, :], st6, T, x_stats)

            def x_norm(b, i):
                dve.wait_ge(x_rstd, b + 1)
                for t in (2 * i, 2 * i + 1):
                    ins = dve.tensor_scalar(xn[:, t, :], x_in[:, T * b + t, :], mvx[:, t, 0:1],
                                            rx[:, t:t + 1], ALU.subtract, ALU.mult)
                ins.then_inc(xn_ready, 1)

            def xn_low(c):
                def step(b):
                    ps = await_fill(f"xt{c}", b)
                    dve.wait_ge(xnT_hi_ready, 2 * b + c + 1)
                    dve.tensor_tensor(xnT_lo[:, c, :], ps[:], xnT_hi[:, c, :], ALU.subtract).then_inc(xnT_ready, 1)
                return step

            def projected_low(name, m):
                def step(b):
                    ps = await_fill(f"{name}{m}", b)
                    i, hi, lo = (0, q_hi, q_lo) if name == "q" else (1, k_hi, k_lo)
                    dve.wait_ge(qk_hi_ready, 4 * b + 2 * m + i + 1)
                    dve.scalar_tensor_tensor(out=lo[:, b % 2, m, :], in0=ps[:], scalar=bias_qk[:, i, m:m + 1],
                                             in1=hi[:, b % 2, m, :], op0=ALU.add,
                                             op1=ALU.subtract).then_inc(qk_ready, 1)
                return step

            def values(name, t0):
                def step(b):
                    ps = await_fill(name, b)
                    for t in (t0, t0 + 1):
                        ins = dve.tensor_tensor(
                            V[:, b % 2, t, :, 0:DH],
                            ps[:, (t - t0) * F:(t - t0 + 1) * F].rearrange("p (h d) -> p h d", h=H),
                            bv_rows[:].rearrange("p (h d) -> p h d", h=H), ALU.add)
                    ins.then_inc(v_ready, 1)
                return step

            def row_max(g):
                dve.wait_ge(scores_ready, g + 1)
                dve.tensor_reduce(nmax[:, g % 8:g % 8 + 1], psS[g % NS][:], AX.X, ALU.max,
                                  negate=True).then_inc(max_ready, 1)

            def copy_turned(g):
                dve.wait_ge(turned, g + 1)
                if g >= 4:
                    dve.wait_ge(pv_done, g - 3)
                dve.tensor_copy(probsT[:, g % 4, :], psT[:]).then_inc(turned_dve, 1)

            def head_norm(n):
                dve.wait_ge(pv_done, H * n + H)
                o = psV[n % 2][:, 0:H * (DH + 1)].rearrange("p (h d) -> p h d", h=H)
                chain(dve.reciprocal(rsum[:, n % 2, :], o[:, :, DH]))
                at = next(n - n0 for n0, size in GROUPS if n0 <= n < n0 + size)
                dve.tensor_tensor(feats[:, at, :].rearrange("p (h d) -> p h d", h=H), o[:, :, 0:DH],
                                  rsum[:, n % 2, :].unsqueeze(2).broadcast_to([P, H, DH]),
                                  ALU.mult).then_inc(feats_ready, 1)

            def attn_copy(j):
                size = GROUPS[j][1]
                ps = await_fill("o", j)
                if j >= 1:
                    dve.wait_ge(x1_ready, j)
                dve.tensor_tensor(attn[:, 0:size, :], ps[:, 0:size * F].rearrange("p (t f) -> p t f", t=size),
                                  bo_rows[:].unsqueeze(1).broadcast_to([P, size, F]),
                                  ALU.add).then_inc(o_copied, 1)

            def attn_statistics(j):
                n, size = GROUPS[j]
                dve.wait_ge(o_copied, j + 1)
                for t in range(size):
                    ins = dve.bn_stats(st6a[:, t, :], attn[:, t, :])
                chain(ins)
                aggregate(lambda t: mva[:, n + t, :], st6a, size, a_stats)

            def residual(j):
                n, size = GROUPS[j]
                dve.wait_ge(a_rstd, j + 1)
                for i in range(size):
                    ins = dve.scalar_tensor_tensor(out=x1[:, n + i, :], in0=attn[:, i, :],
                                                   scalar=ra[:, n + i:n + i + 1], in1=x_in[:, n + i, :],
                                                   op0=ALU.mult, op1=ALU.add)
                ins.then_inc(x1_ready, 1)

            def x1_statistics(j):
                n, size = GROUPS[j]
                dve.wait_ge(x1_ready, j + 1)
                for t in range(size):
                    ins = dve.bn_stats(st61[:, t, :], x1[:, n + t, :])
                chain(ins)
                aggregate(lambda t: mv1[:, n + t, :], st61, size, x1_stats)

            def choose(j):
                n, size = GROUPS[j]
                ps = await_fill("key", j)
                ks = keys[:, 0:size, :]
                dve.tensor_tensor(ks, ps[:, 0:size * NTILE].rearrange("p (t n) -> p t n", t=size),
                                  tie.unsqueeze(1).broadcast_to([P, size, NTILE]), ALU.add).then_inc(key_copied, 1)
                dve.wait_ge(key_copied, j + 1)
                chain(dve.tensor_reduce(kmax[:, 0:size], ks, AX.X, ALU.max))
                dve.tensor_tensor(onehot[:, n:n + size, :], ks,
                                  kmax[:, 0:size].unsqueeze(2).broadcast_to([P, size, NTILE]),
                                  ALU.is_equal).then_inc(onehot_ready, 1)
                dve.wait_ge(onehot_ready, j + 1)
                dve.tensor_scalar(far[:, j % 2, 0:size, :], onehot[:, n:n + size, :], -2 * FAR, FAR, ALU.mult, ALU.add)

            def picked_features(j):
                n, size = GROUPS[j]
                dve.wait_ge(picked, j + 1)
                dve.tensor_reduce(nsl[:, n:n + size, :], pick[:, 0:size, :].rearrange("p t (n j) -> p t j n", j=DS),
                                  AX.X, ALU.add).then_inc(nsl_ready, 1)

            def extremes(j):
                n, size = GROUPS[j]
                r = slice(n, n + size)
                dve.wait_ge(nsl_ready, j + 1)
                dve.wait_ge(gathered, j + 1)
                chain(dve.tensor_tensor(xsl[:, r, :], nsl[:, r, :], G[:, r, TBE:TBE + DS], ALU.mult))
                chain(dve.tensor_tensor(xsl[:, r, :], xsl[:, r, :], G[:, r, TBT:TBT + DS], ALU.add))
                dve.tensor_reduce(tmn[:, 0, 0:size], xsl[:, r, :], AX.X, ALU.min)
                chain(dve.tensor_reduce(tmn[:, 1, 0:size], xsl[:, r, :], AX.X, ALU.max, negate=True))
                for t in range(size):
                    for e in range(2):
                        ins = dve.scalar_tensor_tensor(out=acc[:, e, :], in0=far[:, j % 2, t, :],
                                                       scalar=tmn[:, e, t:t + 1], in1=acc[:, e, :],
                                                       op0=ALU.max, op1=ALU.min)
                    if n + t < NT - 1:
                        chain(ins)
                    else:
                        ins.then_inc(acc_ready, 1)

            def attention(s):
                if s < NU:
                    row_max(s)

            def turned_weights(s):
                if 0 <= s - TURN < NU and on_dve(s - TURN):
                    copy_turned(s - TURN)

            def low_parts(_):
                for n, f in (("q", 0.5), ("k", 1.0), ("v", 1.0)):
                    dve.wait_ge(w_loaded[n], 16)
                    dve.wait_ge(w_hi_ready[n], 1)
                    dve.scalar_tensor_tensor(out=W_lo[n][:].rearrange("p c f -> p (c f)"),
                                             in0=W[n][:].rearrange("p c f -> p (c f)"), scalar=f,
                                             in1=W_hi[n][:].rearrange("p c f -> p (c f)"),
                                             op0=ALU.mult, op1=ALU.subtract).then_inc(w_lo_ready[n], 1)
                dve.wait_ge(bias_ready, 1)
                dve.wait_ge(bv_loaded, 16)

            def route_signs(_):
                dve.wait_ge(slp_loaded, 16)
                dve.tensor_reduce(ssum[:], slp[:], AX.X, ALU.add).then_inc(ssum_ready, 1)
                dve.wait_ge(consts_loaded, 16)
                dve.tensor_copy(ident_b[:], ident).then_inc(ident_b_ready, 1)
                dve.wait_ge(bo_loaded, 16)

            def route_matrix(_):
                dve.wait_ge(ssgn_ready, 1)
                for c in range(KC):
                    ins = dve.tensor_scalar(route[:, c, :], rmask[:, c, :], ssgn[:, c:c + 1], None, ALU.mult)
                ins.then_inc(route_ready, 1)

            dve.memset(acc[:], FAR)
            tasks = [(H * n + H - 1 + WEIGH + NORM, head_norm, (n,)) for n in range(NT)]
            tasks += post(O_COPY, attn_copy) + post(ATTN_STATS, attn_statistics)
            tasks += post(RESIDUAL, residual) + post(X1_STATS, x1_statistics)
            tasks += post(CHOOSE, choose) + post(PICKED, picked_features) + post(EXTREMES, extremes)
            tasks += [(X_STATS[1], low_parts, (0,)), (0, route_signs, (0,)), (1, route_matrix, (0,))]
            tasks += [(UB * b + X_STATS[i], x_statistics, (b, i)) for b in range(NB) for i in range(2)]
            tasks += [(UB * b + X_NORM[i], x_norm, (b, i)) for b in range(NB) for i in range(2)]
            tasks += prep("xt0", xn_low(0)) + prep("xt1", xn_low(1))
            for m in range(KC):
                tasks += prep(f"q{m}", projected_low("q", m)) + prep(f"k{m}", projected_low("k", m))
            tasks += prep("va", values("va", 0)) + prep("vb", values("vb", 2))
            run(attention, tasks, turned_weights)

            dve.wait_ge(accT_ready, 1)
            chain(dve.tensor_reduce(tmm[:], psT[0:NTILE, 0:2 * P].rearrange("p (e n) -> p e n", e=2),
                                    AX.X, ALU.min))
            chain(dve.tensor_copy(tmm_b[0][:], tmm[:]))
            chain(dve.tensor_tensor(tmm_rest[:], tmm[:], tmm_b[0][:], ALU.subtract))
            chain(dve.tensor_copy(tmm_b[1][:], tmm_rest[:]))
            dve.tensor_tensor(tmm_b[2][:], tmm_rest[:], tmm_b[1][:], ALU.subtract).then_inc(tmm_ready, 1)
            dve.wait_ge(lohi_filled, 1)
            chain(dve.tensor_copy(lohi[:], psS[0][:, 0:2 * NT].rearrange("p (n e) -> p n e", e=2)))
            chain(dve.scalar_tensor_tensor(out=rden[:], in0=lohi[:, :, 1], scalar=-1.0,
                                           in1=lohi[:, :, 0], op0=ALU.mult, op1=ALU.subtract))
            chain(dve.tensor_scalar(rden[:], rden[:], 1e-8, None, ALU.add))
            dve.reciprocal(rden[:], rden[:])
            chain(dve.tensor_tensor(u16[:], xsl[:], lohi[:, :, 0].unsqueeze(2).broadcast_to([P, NT, DS]),
                                    ALU.subtract))
            chain(dve.tensor_tensor(u16[:], u16[:], rden[:].unsqueeze(2).broadcast_to([P, NT, DS]), ALU.mult))
            chain(dve.tensor_scalar(u16[:], u16[:], 0.0, 1.0 - 1e-6, ALU.max, ALU.min))
            chain(dve.tensor_scalar(u16[:], u16[:], float(GRID), None, ALU.mult))
            chain(dve.tensor_scalar(gi[:], u16[:], MAGIC, MAGIC, ALU.add, ALU.subtract))
            chain(dve.tensor_tensor(over[:], gi[:], u16[:], ALU.is_gt))
            chain(dve.tensor_tensor(gi[:], gi[:], over[:], ALU.subtract))
            dve.tensor_tensor(xloc[:], u16[:], gi[:], ALU.subtract)

            def evaluate(k, n0, size):
                r = slice(n0, n0 + size)
                pc = piece[:, 0:size * DS, :]
                ht = hit[:, 0:size]
                chain(dve.tensor_tensor(pc, gi[:, r, :].rearrange("p n j -> p (n j)").unsqueeze(2)
                                        .broadcast_to([P, size * DS, GRID]),
                                        steps16.unsqueeze(1).broadcast_to([P, size * DS, GRID]), ALU.is_equal))
                pcf = pc.rearrange("p (n j) g -> p n (j g)", j=DS)
                for e in range(2):
                    ins = dve.tensor_tensor(ht[:, :, e * DS:(e + 1) * DS, :].rearrange("p n j g -> p n (j g)"),
                                            G[:, r, e * DS * GRID:(e + 1) * DS * GRID], pcf, ALU.mult)
                chain(ins)
                chain(dve.tensor_reduce(coef[:, r, :], ht, AX.X, ALU.add))
                chain(dve.tensor_tensor(delta[:, r, :], coef[:, r, DS:2 * DS], xloc[:, r, :], ALU.mult))
                chain(dve.tensor_tensor(delta[:, r, :], delta[:, r, :], coef[:, r, 0:DS], ALU.add))
                chain(dve.tensor_tensor(delta[:, r, :], delta[:, r, :],
                                        G[:, r, TGA:TGA + 1].broadcast_to([P, size, DS]), ALU.mult))
                dve.tensor_reduce(s1[:, r], delta[:, r, :], AX.X, ALU.add)
                chain(dve.tensor_tensor(sq[:, r, :], nsl[:, r, :],
                                        sy[:, r].unsqueeze(2).broadcast_to([P, size, DS]), ALU.mult))
                chain(dve.scalar_tensor_tensor(out=sq[:, r, :], in0=sq[:, r, :], scalar=2.0, in1=delta[:, r, :],
                                               op0=ALU.mult, op1=ALU.add))
                dve.tensor_scalar(s1[:, r], s1[:, r], 1.0 / F, None, ALU.mult)
                chain(dve.tensor_tensor(sq[:, r, :], sq[:, r, :], delta[:, r, :], ALU.mult))
                dve.tensor_tensor(c0[:, r], s1[:, r], s1[:, r], ALU.mult)
                chain(dve.tensor_reduce(s2[:, r], sq[:, r, :], AX.X, ALU.add))
                chain(dve.scalar_tensor_tensor(out=s2[:, r], in0=s2[:, r], scalar=1.0 / F, in1=vy[:, r],
                                               op0=ALU.mult, op1=ALU.add))
                dve.scalar_tensor_tensor(out=s2[:, r], in0=s2[:, r], scalar=EPS, in1=c0[:, r],
                                         op0=ALU.add, op1=ALU.subtract).then_inc(var3_ready, 1)

            def constants(k, n0, size):
                r = slice(n0, n0 + size)
                dve.wait_ge(r3_ready, k + 1)
                dve.tensor_tensor(delta[:, r, :], delta[:, r, :],
                                  r3[:, r].unsqueeze(2).broadcast_to([P, size, DS]), ALU.mult)
                chain(dve.tensor_tensor(c1[:, r], r1[:, r], r3[:, r], ALU.mult))
                dve.tensor_tensor(s1[:, r], s1[:, r], r3[:, r], ALU.mult)
                dve.tensor_tensor(s2[:, r], mva[:, r, 0], ra[:, r], ALU.mult)
                chain(dve.tensor_tensor(c0[:, r], nm1[:, r], c1[:, r], ALU.mult))
                chain(dve.tensor_tensor(c0[:, r], c0[:, r], s1[:, r], ALU.subtract))
                chain(dve.tensor_tensor(c0[:, r], c0[:, r], s2[:, r], ALU.subtract))
                dve.tensor_scalar(c1[:, r], c1[:, r], 1.0, None, ALU.add).then_inc(c_ready, 1)

            def finish(n0, size):
                for n in range(n0, n0 + size):
                    if not by_pool(n):
                        spread(dve, n).then_inc(put_dve, 1)
                for n in range(n0, n0 + size):
                    dve.wait_ge(rows_ready, n + 1)
                    if by_pool(n):
                        dve.wait_ge(put_ready, (n + 1) // 3)
                    else:
                        dve.wait_ge(put_dve, n + 1 - (n + 1) // 3)
                    ins = dve.tensor_tensor(res[:, n, :], rows_b[:, n, :], put[:, n, :], ALU.add)
                    if n % 2:
                        ins.then_inc(res_ready, 1)

            dve.wait_ge(scales_ready, len(GROUPS))
            for k, (n0, size) in enumerate(CHUNKS):
                evaluate(k, n0, size)
            for k, (n0, size) in enumerate(CHUNKS):
                constants(k, n0, size)
                finish(n0, size)

        @block.tensor
        def _(pe):
            def fill(name, emit, source):
                def step(i):
                    at = ORDER[name, i]
                    if at >= 2:
                        pe.wait_ge(*copied_out(FILLS[at - 2][1], FILLS[at - 2][2]))
                    pe.wait_ge(*source(i))
                    emit(psX[at % 2], i).then_inc(filled[at % 2], 1)
                return step

            def turn_xn(c):
                def emit(ps, b):
                    for t in range(T):
                        ins = pe.transpose(ps[:, t * P:(t + 1) * P], xn[:, t, c * P:(c + 1) * P], ident)
                    return ins
                return emit

            def parts(out, a_hi, a_lo, b_hi, b_lo, first, last):
                pe.matmul(out, a_hi, b_lo, start=first, stop=False)
                pe.matmul(out, a_lo, b_hi, start=False, stop=False)
                return pe.matmul(out, a_hi, b_hi, start=False, stop=last)

            def project(name, m):
                cols = slice(m * P, (m + 1) * P)

                def emit(ps, b):
                    if b == 0 and m == 0:
                        pe.wait_ge(w_lo_ready[name], 1)
                    for c in range(KC):
                        ins = parts(ps[:], W_hi[name][:, c, cols], W_lo[name][:, c, cols],
                                    xnT_hi[:, c, :], xnT_lo[:, c, :], c == 0, c == KC - 1)
                    return ins
                return emit

            def project_v(t0):
                def emit(ps, b):
                    if b == 0 and t0 == 0:
                        pe.wait_ge(w_lo_ready["v"], 1)
                    for t in (t0, t0 + 1):
                        rows = slice(t * P, (t + 1) * P)
                        for c in range(KC):
                            ins = parts(ps[:, (t - t0) * F:(t - t0 + 1) * F], xnT_hi[:, c, rows],
                                        xnT_lo[:, c, rows], W_hi["v"][:, c, :], W_lo["v"][:, c, :],
                                        c == 0, c == KC - 1)
                    return ins
                return emit

            def turn_feats(ps, j):
                for i in range(GROUPS[j][1]):
                    for c in range(KC):
                        ins = pe.transpose(ps[:, i * F + c * P:i * F + (c + 1) * P],
                                           feats[:, i, c * P:(c + 1) * P], ident)
                return ins

            def project_o(ps, j):
                if j == 0:
                    pe.wait_ge(w_loaded["o"], 16)
                for i in range(GROUPS[j][1]):
                    for c in range(KC):
                        ins = pe.matmul(ps[:, i * F:(i + 1) * F], featsT[:, i, c, :], W["o"][:, c, :],
                                        start=(c == 0), stop=(c == KC - 1))
                return ins

            def turn_yn(ps, j):
                for c in range(KC):
                    for i in range(GROUPS[j][1]):
                        ins = pe.transpose(ps[:, (c * GT + i) * P:(c * GT + i + 1) * P],
                                           yn[:, i, c * P:(c + 1) * P], ident)
                return ins

            def key_sums(ps, j):
                if j == 0:
                    pe.wait_ge(route_ready, 1)
                for i in range(GROUPS[j][1]):
                    for c in range(KC):
                        ins = pe.matmul(ps[:, i * NTILE:(i + 1) * NTILE], signT[:, c, i * P:(i + 1) * P],
                                        route[:, c, :], start=(c == 0), stop=(c == KC - 1))
                return ins

            def turn_onehot(ps, j):
                n, size = GROUPS[j]
                if j == 0:
                    pe.wait_ge(ident_b_ready, 1)
                for i in range(size):
                    ins = pe.transpose(ps[0:NTILE, :].bitcast(BF16)[:, i * P:(i + 1) * P],
                                       onehot[:, n + i, :], ident_b[:])
                return ins

            def gather_rows(ps, j):
                n, size = GROUPS[j]
                if j == 0:
                    pe.wait_ge(table_ready, 1)
                for i in range(size):
                    for k in (2, 1, 0):
                        ins = pe.matmul(ps[:, i * TW:(i + 1) * TW], onehotT[:, n + i, :], table_b[k][:],
                                        start=(k == 2), stop=(k == 0))
                return ins

            def scores(g):
                b, h, t = g // UB, g % H, g % UB // H
                if t == 0 and h % 2 == 0:
                    pe.wait_ge(qk_ready, 4 * b + h + 2)
                if g >= NS:
                    pe.wait_ge(probs_ready, g - NS + 1)
                rows = slice(DH * (h % 2), DH * (h % 2) + DH)
                m, qs = h // 2, slice(t * P, (t + 1) * P)
                parts(psS[g % NS][:], q_hi[rows, b % 2, m, qs], q_lo[rows, b % 2, m, qs],
                      k_hi[rows, b % 2, m, :], k_lo[rows, b % 2, m, :], True, True).then_inc(scores_ready, 1)

            def copied(g):
                if on_dve(g):
                    pe.wait_ge(turned_dve, g // 4 + 1)
                else:
                    pe.wait_ge(turned_act, (g + 1) - (g + 1) // 4)

            def transposes(g):
                pe.wait_ge(probs_ready, g + 1)
                if g >= 1:
                    copied(g - 1)
                for k in range(T):
                    ins = pe.transpose(psT[:, k * P:(k + 1) * P], probs[:, g % 4, k * P:(k + 1) * P], ident)
                ins.then_inc(turned, 1)

            def weighted(g):
                b, h, n = g // UB, g % H, g // H
                copied(g)
                if g % UB == 0:
                    pe.wait_ge(v_ready, 2 * b + 2)
                if h == 0 and n >= 2:
                    pe.wait_ge(feats_ready, n - 1)
                for k in range(T):
                    ins = pe.matmul(psV[n % 2][:, h * (DH + 1):(h + 1) * (DH + 1)],
                                    probsT[:, g % 4, k * P:(k + 1) * P], V[:, b % 2, k, h, :],
                                    start=(k == 0), stop=(k == T - 1))
                ins.then_inc(pv_done, 1)

            def attention(s):
                if s < NU:
                    scores(s)
                if 0 <= s - WEIGH < NU:
                    weighted(s - WEIGH)
                if 0 <= s - TURN < NU:
                    transposes(s - TURN)

            def by_batch(s, per):
                return lambda b: (s, per * (b + 1))

            def by_group(s):
                return lambda j: (s, j + 1)

            steps = {
                "xt0": fill("xt0", turn_xn(0), by_batch(xn_ready, 2)),
                "xt1": fill("xt1", turn_xn(1), by_batch(xn_ready, 2)),
                "va": fill("va", project_v(0), by_batch(xnT_ready, 2)),
                "vb": fill("vb", project_v(2), by_batch(xnT_ready, 2)),
                "ft": fill("ft", turn_feats, lambda j: (feats_ready, sum(GROUPS[j]))),
                "o": fill("o", project_o, by_group(featsT_ready)),
                "yt": fill("yt", turn_yn, by_group(yn_ready)),
                "key": fill("key", key_sums, by_group(sign_ready)),
                "oht": fill("oht", turn_onehot, by_group(onehot_ready)),
                "ga": fill("ga", gather_rows, by_group(onehotT_ready)),
            }
            for m in range(KC):
                for name in "qk":
                    steps[f"{name}{m}"] = fill(f"{name}{m}", project(name, m), by_batch(xnT_ready, 2))

            pe.wait_ge(consts_loaded, 16)
            pe.wait_ge(ones_set, 1)
            run(attention, [(at, steps[name], (i,)) for at, name, i in FILLS])

            pe.wait_ge(acc_ready, 1)
            for e in range(2):
                ins = pe.transpose(psT[0:NTILE, e * P:(e + 1) * P], acc[:, e, :], ident)
            ins.then_inc(accT_ready, 1)
            pe.wait_ge(tmm_ready, 1)
            for n in range(NT):
                for k in (2, 1, 0):
                    ins = pe.matmul(psS[0][:, 2 * n:2 * n + 2], onehotT[:, n, :], tmm_b[k][:],
                                    start=(k == 2), stop=(k == 0))
            ins.then_inc(lohi_filled, 1)


_INS = ["L0_attn_x", "L0_attn_Wq", "L0_attn_bq", "L0_attn_Wk", "L0_attn_bk", "L0_attn_Wv", "L0_attn_bv",
        "L0_attn_Wo", "L0_attn_bo", "L0_ffn_ln_gamma", "L0_ffn_ln_beta", "L0_ffn_spline_bases",
        "L0_ffn_spline_slopes", "L0_ffn_output_scale"]


def shape_constants(np):
    c = np.zeros((P, CW), np.float32)
    c[:, 0:P] = np.eye(P)
    feature = np.arange(KC)[None, :, None] * P + np.arange(P)[:, None, None]
    tile = np.arange(NTILE)[None, None, :]
    mask = (1024 * (feature // (F // NCL) == tile // (NTILE // NCL)) + 8 * (feature // DS == tile))
    c[:, P:P + KC * NTILE] = mask.reshape(P, KC * NTILE)
    n = np.arange(NTILE)
    c[:, P + KC * NTILE:P + KC * NTILE + NTILE] = 128 * (NCL - 1 - n // NCL) + (NCL - 1 - n % NCL)
    c[:, P + KC * NTILE + NTILE:] = np.arange(GRID)
    return c


def kernel(**inputs):
    import numpy as _np
    import concourse.bacc as _bacc
    from concourse.bass_utils import run_bass_kernel_spmd as _run

    nc = _bacc.Bacc("TRN2", target_bir_lowering=False, num_devices=1)
    arrays = {f"in_{n}": _np.ascontiguousarray(inputs[n]) for n in _INS}
    arrays["in_shape_constants"] = shape_constants(_np)
    args = [nc.dram_tensor(n, a.shape, mybir.dt.from_np(a.dtype), kind="ExternalInput").ap()
            for n, a in arrays.items()]
    args.append(nc.dram_tensor("out_dram", (NB, SEQ, F), F32, kind="ExternalOutput").ap())
    sandwich(nc, *args)
    r = _run(nc, [arrays], core_ids=[0])
    return r.results[0]["out_dram"]
```

```python
from contextlib import ExitStack

import concourse.bass as bass
from concourse import mybir

F32 = mybir.dt.float32
I32 = mybir.dt.int32
F32R = mybir.dt.float32r
BF16 = mybir.dt.bfloat16
ALU = mybir.AluOpType
ACT = mybir.ActivationFunctionType
AX = mybir.AxisListType

P = 128
NB, SEQ, F = 4, 512, 256
T = SEQ // P
NT = NB * T
KC = F // P
H, DH = 4, 64
UB = H * T
NU = NB * UB
NTILE, DS, GRID = 64, 4, 16
NCL = 8
EPS = 1e-5
BELOW_ONE = 1.0 - 17 * 2.0 ** -24
FAR = 1e38
TW = 2 * DS * GRID + 1 + 2 * DS
TG, TS, TGA, TBE = 0, DS * GRID, 2 * DS * GRID, 2 * DS * GRID + 1
TBT = TBE + DS
CW = P + KC * NTILE + NTILE

GROUPS = [(n, 2) for n in range(0, NT - 2, 2)] + [(NT - 2, 1), (NT - 1, 1)]
N_GROUPS = len(GROUPS)
N_LATE = 4
LAST_FEW = 2
GT = 2
PARTS = [(0, 6), (6, NT - 6)]
SPREAD_FIRST = 3
BY_POOL = 9
WARM_UP = 20
TURN = 4
WEIGH = 6
NS, NX = 2, 3
NP = 5

PREP = {"xt0": -12, "xt1": -12, "q0": -10, "k0": -9, "q1": -7, "k1": -5, "va": -4, "vb": -2}
FIRST_PREP = {"xt0": -12, "xt1": -11, "q0": -10, "k0": -9, "q1": -8, "k1": 0, "va": 1, "vb": 3}
X_STATS = (-16, -15)
X_NORM = (-13, -13)
START = {"low_q": -12, "low_k": -12, "low_v": -8, "low_o": 4, "biases": -12, "table": 0, "route_signs": 0,
         "slope_signs": 1, "route": 1, "high_o": 3}
FILLING = ("ft", "o", "yt", "key", "oht", "ga")
POST = {"ft": 2, "o": 4, "stats": 6, "residual": 8, "x1_stats": 9, "yn": 10, "yt": 12, "key": 14,
        "oht": 17, "ga": 18, "picked": 17, "later": 19, "extremes": 19}
LATE_POST = {"ft": 1, "o": 3, "stats": 5, "residual": 7, "x1_stats": 8, "yn": 10, "yt": 12, "key": 13,
             "oht": 16, "ga": 17, "picked": 17, "later": 19, "extremes": 18}


def base_slot(j):
    n, size = GROUPS[j]
    return (n + size) * H - 1 + WEIGH


def post_slot(name, j):
    at = base_slot(j) + (POST if j < len(GROUPS) - N_LATE else LATE_POST)[name]
    return max(at, post_slot(name, j - 1)) if j else at


def all_fills():
    fills = [(UB * b + at, name, b) for b in range(NB) for name, at in (PREP if b else FIRST_PREP).items()]
    fills += [(post_slot(name, j), name, j) for j in range(len(GROUPS)) for name in FILLING]
    return sorted(fills, key=lambda f: f[0])


FILLS = all_fills()
ORDER = {(name, i): at for at, (_, name, i) in enumerate(FILLS)}


def all_steps():
    steps = [(H * n + H + WEIGH, "heads", n) for n in range(NT)]
    for name in ("stats", "residual", "x1_stats", "yn", "picked", "later", "extremes"):
        steps += [(post_slot(name, j), name, j) for j in range(N_GROUPS)]
    steps += [(at, name, 0) for name, at in START.items()]
    for b in range(NB):
        for i in range(2):
            steps += [(UB * b + X_STATS[i], f"x_stats{i}", b), (UB * b + X_NORM[i], f"x_norm{i}", b)]
    return sorted(steps, key=lambda step: step[0])


STEPS = all_steps()
SLOTS = range(STEPS[0][0], STEPS[-1][0] + 1)


def fills_at(s):
    return [(name, i) for at, name, i in FILLS if at == s]


def steps_at(s):
    return [(name, i) for at, name, i in STEPS if at == s]


def bank_of(name, i):
    return ORDER[name, i] % NX


def filled_count(name, i):
    return ORDER[name, i] // NX + 1


def on_dve(g):
    return g % 16 in (3, 7, 11)


def sandwich(nc, x, wq, bq, wk, bk, wv, bv, wo, bo, gamma, beta, bases, slopes, oscale, consts, out):
    with ExitStack() as ctx:
        def sb(name, shape, dt=F32):
            return ctx.enter_context(nc.sbuf_tensor(name, shape, dt))

        def sem(name):
            return ctx.enter_context(nc.semaphore(name))

        x_in = sb("x_in", [P, NT, F])
        x1 = sb("x1", [P, NT, F])
        xn = sb("xn", [P, T, F])
        xnT_hi, xnT_lo = sb("xnT_hi", [P, KC, SEQ], F32R), sb("xnT_lo", [P, KC, SEQ], F32R)
        W = {n: sb("w" + n, [P, KC, F]) for n in "qkvo"}
        W_hi = {n: sb(f"w{n}_hi", [P, KC, F], F32R) for n in "qkvo"}
        W_lo = {n: sb(f"w{n}_lo", [P, KC, F], F32R) for n in "qkvo"}
        bqk = sb("bqk", [P, 2, KC])
        bias_qk = sb("bias_qk", [P, 2, KC])
        bv_rows = sb("bv_rows", [P, F])
        bo_rows = sb("bo_rows", [P, F])
        gbT = sb("gbT", [P, 2, KC])
        cst = sb("cst", [P, CW])
        ident_b = sb("ident_b", [P, P], BF16)
        q_hi, q_lo = sb("q_hi", [P, 2, KC, SEQ], F32R), sb("q_lo", [P, 2, KC, SEQ], F32R)
        k_hi, k_lo = sb("k_hi", [P, 2, KC, SEQ], F32R), sb("k_lo", [P, 2, KC, SEQ], F32R)
        V = sb("V", [P, 2, T, H, DH + 1])
        probs = sb("probs", [P, NP, SEQ])
        probsT = sb("probsT", [P, NP, SEQ])
        nmax = sb("nmax", [P, 8])
        rsum = sb("rsum", [P, 2, H])
        feats = sb("feats", [P, GT, F])
        featsT_hi, featsT_lo = sb("featsT_hi", [P, GT, KC, P], F32R), sb("featsT_lo", [P, GT, KC, P], F32R)
        attn = sb("attn", [P, GT, F])
        yn = sb("yn", [P, 2, GT, F])
        signT = sb("signT", [P, KC, GT * P], BF16)
        route = sb("route", [P, KC, NTILE], BF16)
        slp = sb("slp", [P, KC, GRID])
        ssum = sb("ssum", [P, KC])
        ssgn = sb("ssgn", [P, KC])
        tie_b = sb("tie_b", [2, NTILE], BF16)
        ones_b = sb("ones_b", [2, P], BF16)
        kmax = sb("kmax", [P, GT])
        onehot = sb("onehot", [P, NT, NTILE], BF16)
        onehotT = sb("onehotT", [NTILE, NT, P], BF16)
        table = sb("table", [NTILE, TW])
        table_rest = sb("table_rest", [NTILE, TW])
        table_b = [sb(f"table_b{i}", [NTILE, TW], BF16) for i in range(3)]
        G = sb("G", [P, NT, TW])
        pick = sb("pick", [P, 2, GT, F])
        far = sb("far", [P, 2, GT, NTILE])
        nsl = sb("nsl", [P, NT, DS])
        xsl = sb("xsl", [P, NT, DS])
        tmn = sb("tmn", [P, 2, GT])
        acc = sb("acc", [P, 2, NTILE])
        st6 = sb("st6", [P, T, 6])
        st6a = sb("st6a", [P, GT, 6])
        st61 = sb("st61", [P, GT, 6])
        mvx = sb("mvx", [P, T, 2])
        rx = sb("rx", [P, T])
        mva = sb("mva", [P, NT, 2])
        ra = sb("ra", [P, NT])
        mv1 = sb("mv1", [P, NT, 2])
        r12 = sb("r12", [P, NT])
        nb12 = sb("nb12", [P, NT])
        nm1 = sb("nm1", [P, NT])
        r1 = sb("r1", [P, NT])
        vy = sb("vy", [P, NT])
        sy = sb("sy", [P, NT])
        vt = [sb(f"vt{i}", [P, NT]) for i in range(5)]
        mhalf = sb("mhalf", [P, NT])
        phalf = sb("phalf", [P, NT])
        tmm = sb("tmm", [NTILE, 2])
        tmm_rest = sb("tmm_rest", [NTILE, 2])
        tmm_b = sb("tmm_b", [NTILE, 3, 2], BF16)
        lohi = sb("lohi", [P, NT, 2])
        rden = sb("rden", [P, NT])
        u16 = sb("u16", [P, NT, DS])
        bit = sb("bit", [P, 2, NT, DS])
        delta = sb("delta", [P, NT, DS])
        sq = sb("sq", [P, NT, DS])
        s1 = sb("s1", [P, NT])
        s2 = sb("s2", [P, NT])
        r3 = sb("r3", [P, NT])
        ym = sb("ym", [P, NT])
        shift = sb("shift", [P, NT])
        c1 = sb("c1", [P, NT])
        c0 = sb("c0", [P, NT])
        rows_b = sb("rows_b", [P, NT, F])
        put = sb("put", [P, NT, F])
        res = x_in

        psS = [ctx.enter_context(nc.psum_tensor(f"psS{i}", [P, SEQ], F32)) for i in range(NS)]
        psT = ctx.enter_context(nc.psum_tensor("psT", [P, SEQ], F32))
        psV = [ctx.enter_context(nc.psum_tensor(f"psV{i}", [P, SEQ], F32)) for i in range(2)]
        psX = [ctx.enter_context(nc.psum_tensor(f"psX{i}", [P, SEQ], F32)) for i in range(NX)]

        ident = cst[:, 0:P]
        rmask = cst[:, P:P + KC * NTILE].rearrange("p (c n) -> p c n", c=KC)
        tie = cst[0:2, P + KC * NTILE:CW]

        x_first_loaded = sem("x_first_loaded")
        x_loaded, consts_loaded, bv_loaded = sem("x_loaded"), sem("consts_loaded"), sem("bv_loaded")
        w_loaded = {n: sem("w_loaded_" + n) for n in "qkvo"}
        w_hi_ready = {n: sem(f"w{n}_hi_ready") for n in "qkvo"}
        w_lo_ready = {n: sem(f"w{n}_lo_ready") for n in "qkvo"}
        bqk_loaded, gbT_loaded, slp_loaded = sem("bqk_loaded"), sem("gbT_loaded"), sem("slp_loaded")
        bo_loaded, table_loaded, stored = sem("bo_loaded"), sem("table_loaded"), sem("stored")
        ones_set, ident_b_ready, table_ready = sem("ones_set"), sem("ident_b_ready"), sem("table_ready")
        bias_ready, ssum_ready, ssgn_ready, route_ready = (sem("bias_ready"), sem("ssum_ready"),
                                                           sem("ssgn_ready"), sem("route_ready"))
        x_stats, x_rstd, xn_ready = sem("x_stats"), sem("x_rstd"), sem("xn_ready")
        filled = [sem(f"filled{i}") for i in range(NX)]
        xnT_hi_ready, xnT_ready = sem("xnT_hi_ready"), sem("xnT_ready")
        qk_hi_ready, qk_ready, v_ready = sem("qk_hi_ready"), sem("qk_ready"), sem("v_ready")
        scores_ready, max_ready, probs_ready = sem("scores_ready"), sem("max_ready"), sem("probs_ready")
        turned, turned_act, turned_dve = sem("turned"), sem("turned_act"), sem("turned_dve")
        featsT_hi_ready = sem("featsT_hi_ready")
        pv_done, feats_ready, featsT_ready = sem("pv_done"), sem("feats_ready"), sem("featsT_ready")
        x1_ready = sem("x1_ready")
        o_copied, a_stats, a_rstd, x1_stats, x1_scale = (sem("o_copied"), sem("a_stats"), sem("a_rstd"),
                                                         sem("x1_stats"), sem("x1_scale"))
        yn_ready, sign_ready, onehot_ready = sem("yn_ready"), sem("sign_ready"), sem("onehot_ready")
        onehotT_ready, picked, gathered = sem("onehotT_ready"), sem("picked"), sem("gathered")
        nsl_ready = sem("nsl_ready")
        acc_ready, accT_ready, tmm_ready, lohi_filled = (sem("acc_ready"), sem("accT_ready"),
                                                         sem("tmm_ready"), sem("lohi_filled"))
        scales_ready, var3_ready, r3_ready, c_ready = (sem("scales_ready"), sem("var3_ready"),
                                                       sem("r3_ready"), sem("c_ready"))
        rows_ready, put_ready, put_dve, res_ready = (sem("rows_ready"), sem("put_ready"), sem("put_dve"),
                                                     sem("res_ready"))
        dve_chain, pool_chain = sem("dve_chain"), sem("pool_chain")

        def copied_out(name, i):
            return {"xt0": (xnT_ready, 2 * i + 1), "xt1": (xnT_ready, 2 * i + 2),
                    "q0": (qk_ready, 4 * i + 1), "k0": (qk_ready, 4 * i + 2),
                    "q1": (qk_ready, 4 * i + 3), "k1": (qk_ready, 4 * i + 4),
                    "va": (v_ready, 2 * i + 1), "vb": (v_ready, 2 * i + 2),
                    "ft": (featsT_ready, i + 1), "o": (o_copied, i + 1), "yt": (sign_ready, i + 1),
                    "key": (onehot_ready, i + 1), "oht": (onehotT_ready, i + 1), "ga": (gathered, i + 1)}[name]

        class Chain:

            def __init__(self, eng, s):
                self.eng, self.s, self.n = eng, s, 0

            def mark(self, ins):
                self.n += 1
                ins.then_inc(self.s, 1)
                return self.n

            def after(self, n):
                self.eng.wait_ge(self.s, n)

            def __call__(self, ins):
                self.after(self.mark(ins))

        def spread(eng, n):
            return eng.tensor_tensor(put[:, n, :].rearrange("p (n j) -> p n j", j=DS),
                                     onehot[:, n, :].unsqueeze(2).broadcast_to([P, NTILE, DS]),
                                     delta[:, n:n + 1, :].broadcast_to([P, NTILE, DS]), ALU.mult)

        block = ctx.enter_context(nc.Block())

        @block.sync
        def _(sp):
            def load_x(b):
                sp.dma_start(x_in[:, T * b:T * b + T],
                             x[b].rearrange("(p t) f -> p t f", t=T)).then_inc(x_loaded, 16)

            x0 = x[0].rearrange("(p t) f -> p t f", t=T)
            sp.dma_start(x_in[:, 0:2], x0[:, 0:2]).then_inc(x_first_loaded, 16)
            sp.dma_start(x_in[:, 2:T], x0[:, 2:T]).then_inc(x_loaded, 16)
            for n, w in (("q", wq), ("k", wk), ("v", wv)):
                sp.dma_start(W[n][:], w.rearrange("(c p) n -> p c n", p=P)).then_inc(w_loaded[n], 16)
            sp.dma_start(bv_rows[:], bv.unsqueeze(0).broadcast_to([P, F])).then_inc(bv_loaded, 16)
            sp.dma_start(slp[:], slopes.rearrange("(c n) j g -> (n j) c g", c=KC)).then_inc(slp_loaded, 16)
            sp.dma_start(W["o"][:], wo.rearrange("(c p) n -> p c n", p=P)).then_inc(w_loaded["o"], 16)
            sp.dma_start(bo_rows[:], bo.unsqueeze(0).broadcast_to([P, F])).then_inc(bo_loaded, 16)
            with nc.allow_non_contiguous_dma(reason="256 factors, one to a partition"):
                for i, v in enumerate((gamma, beta)):
                    sp.dma_start(gbT[:, i, :], v.rearrange("(c p) -> p c", p=P)).then_inc(gbT_loaded, 16)
            for dst, src in ((table[:, TG:TG + DS * GRID], bases.rearrange("n j g -> n (j g)")),
                             (table[:, TS:TS + DS * GRID], slopes.rearrange("n j g -> n (j g)")),
                             (table[:, TGA:TGA + 1], oscale.unsqueeze(1)),
                             (table[:, TBE:TBE + DS], gamma.rearrange("(n j) -> n j", j=DS)),
                             (table[:, TBT:TBT + DS], beta.rearrange("(n j) -> n j", j=DS))):
                sp.dma_start(dst, src).then_inc(table_loaded, 16)
            for b in range(1, NB):
                sp.wait_ge(x_loaded, 16 * b)
                load_x(b)
            for b in range(NB):
                for i in range(2):
                    sp.wait_ge(res_ready, 2 * b + i + 1)
                    sp.dma_start(out[b].rearrange("(p t) f -> p t f", t=T)[:, 2 * i:2 * i + 2],
                                 res[:, T * b + 2 * i:T * b + 2 * i + 2]).then_inc(stored, 16)
            sp.wait_ge(stored, 16 * 2 * NB)

        @block.gpsimd
        def _(pool):
            chain = Chain(pool, pool_chain)

            def x_scale(b):
                pool.wait_ge(x_stats, b + 1)
                chain(pool.tensor_scalar(vt[0][:, 0:T], mvx[:, :, 1], EPS, None, ALU.add))
                pool.tensor_tensor(rx[:], vt[0][:, 0:T], mhalf[:, 0:T], ALU.pow).then_inc(x_rstd, 1)

            def attn_scale(j):
                n, size = GROUPS[j]
                r = slice(n, n + size)
                pool.wait_ge(a_stats, j + 1)
                chain(pool.tensor_scalar(vt[1][:, r], mva[:, r, 1], EPS, None, ALU.add))
                pool.tensor_tensor(ra[:, r], vt[1][:, r], mhalf[:, r], ALU.pow).then_inc(a_rstd, 1)

            def yn_scale(j):
                n, size = GROUPS[j]
                r = slice(n, n + size)
                pool.wait_ge(x1_stats, j + 1)
                chain(pool.tensor_scalar(vt[2][:, r], mv1[:, r, 1], 1.0 + EPS, EPS * EPS, ALU.mult, ALU.add))
                if j < N_GROUPS - LAST_FEW:
                    chain(pool.tensor_tensor(r12[:, r], vt[2][:, r], mhalf[:, r], ALU.pow))
                    chain(pool.tensor_scalar(nm1[:, r], mv1[:, r, 0], -1.0, None, ALU.mult))
                    pool.tensor_tensor(nb12[:, r], nm1[:, r], r12[:, r], ALU.mult).then_inc(x1_scale, 1)
                else:
                    pool.tensor_tensor(r12[:, r], vt[2][:, r], mhalf[:, r], ALU.pow).then_inc(x1_scale, 1)
                    chain(pool.tensor_scalar(nm1[:, r], mv1[:, r, 0], -1.0, None, ALU.mult))

            def later_scales(n, size):
                r = slice(n, n + size)
                chain(pool.tensor_scalar(vt[3][:, r], mv1[:, r, 1], EPS, None, ALU.add))
                chain(pool.tensor_tensor(r1[:, r], vt[3][:, r], mhalf[:, r], ALU.pow))
                chain(pool.tensor_tensor(vt[4][:, r], r1[:, r], r1[:, r], ALU.mult))
                chain(pool.tensor_tensor(vy[:, r], vt[4][:, r], mv1[:, r, 1], ALU.mult))
                chain(pool.tensor_scalar(vt[3][:, r], vy[:, r], EPS, None, ALU.add))
                pool.tensor_tensor(ym[:, r], nm1[:, r], r1[:, r], ALU.mult)
                pool.tensor_tensor(shift[:, r], mva[:, r, 0], ra[:, r], ALU.mult)
                pool.tensor_tensor(sy[:, r], vt[3][:, r], phalf[:, r], ALU.pow).then_inc(scales_ready, 1)

            def pick_features(j):
                n, size = GROUPS[j]
                pool.wait_ge(onehot_ready, j + 1)
                if j >= 2:
                    pool.wait_ge(nsl_ready, j - 1)
                for i in range(size):
                    ins = pool.tensor_tensor(pick[:, j % 2, i, :].rearrange("p (n j) -> p n j", j=DS),
                                             yn[:, j % 2, i, :].rearrange("p (n j) -> p n j", j=DS),
                                             onehot[:, n + i, :].unsqueeze(2).broadcast_to([P, NTILE, DS]),
                                             ALU.mult)
                ins.then_inc(picked, 1)

            pool.memset(V[:, :, :, :, DH:DH + 1], 1.0).then_inc(ones_set, 1)
            pool.memset(phalf[:], 0.5)
            chain(pool.memset(mhalf[:], -0.5))

            def split_table():
                pool.wait_ge(table_loaded, 16 * 5)
                chain(pool.tensor_copy(table_b[0][:], table[:]))
                chain(pool.tensor_tensor(table_rest[:], table[:], table_b[0][:], ALU.subtract))
                chain(pool.tensor_copy(table_b[1][:], table_rest[:]))
                pool.tensor_tensor(table_b[2][:], table_rest[:], table_b[1][:],
                                   ALU.subtract).then_inc(table_ready, 1)

            for s in SLOTS:
                for name, i in fills_at(s - 1):
                    if name == "key":
                        pick_features(i)
                for name, i in steps_at(s):
                    if name == "table":
                        split_table()
                    elif name == "x_stats1":
                        x_scale(i)
                    elif name == "stats":
                        attn_scale(i)
                    elif name == "x1_stats":
                        yn_scale(i)
                    elif name == "later" and i < N_GROUPS - N_LATE:
                        later_scales(*GROUPS[i])
            later_scales(GROUPS[-N_LATE][0], NT - GROUPS[-N_LATE][0])
            pool.wait_ge(var3_ready, 1)
            for n0, size in PARTS:
                r = slice(n0, n0 + size)
                pool.tensor_tensor(r3[:, r], s2[:, r], mhalf[:, r], ALU.pow).then_inc(r3_ready, 1)
            for n in range(NT - BY_POOL, NT):
                spread(pool, n).then_inc(put_ready, 1)

        @block.scalar
        def _(act):
            def await_fill(name, i):
                act.wait_ge(filled[bank_of(name, i)], filled_count(name, i))
                return psX[bank_of(name, i)]

            def xn_turned(c):
                def step(b):
                    ps = await_fill(f"xt{c}", b)
                    act.copy(xnT_hi[:, c, :], ps[:]).then_inc(xnT_hi_ready, 1)
                return step

            def projected(name, m):
                def step(b):
                    ps = await_fill(f"{name}{m}", b)
                    i, hi = (0, q_hi) if name == "q" else (1, k_hi)
                    act.activation(hi[:, b % 2, m, :], ps[:], ACT.Identity, bias=bias_qk[:, i, m:m + 1],
                                   scale=1.0).then_inc(qk_hi_ready, 1)
                return step

            def feats_turned(j):
                size = GROUPS[j][1]
                if j >= 1:
                    await_fill("o", j - 1)
                ps = await_fill("ft", j)
                act.copy(featsT_hi[:, 0:size].rearrange("p t c q -> p (t c q)"),
                         ps[:, 0:size * F]).then_inc(featsT_hi_ready, 1)

            def normalize_y(j):
                n, size = GROUPS[j]
                act.wait_ge(x1_scale, j + 1)
                if j >= 2:
                    act.wait_ge(picked, j - 1)
                for i in range(size):
                    ins = act.activation(yn[:, j % 2, i, :], x1[:, n + i, :], ACT.Identity,
                                         bias=nb12[:, n + i:n + i + 1], scale=r12[:, n + i:n + i + 1])
                ins.then_inc(yn_ready, 1)

            def signs(j):
                size = GROUPS[j][1]
                if j >= 1:
                    await_fill("key", j - 1)
                ps = await_fill("yt", j)
                for c in range(KC):
                    ins = act.activation(signT[:, c, 0:size * P], ps[:, c * GT * P:c * GT * P + size * P],
                                         ACT.Sign, bias=gbT[:, 1, c:c + 1], scale=gbT[:, 0, c:c + 1])
                ins.then_inc(sign_ready, 1)

            def onehot_turned(j):
                n, size = GROUPS[j]
                ps = await_fill("oht", j)
                act.copy(onehotT[:, n:n + size, :].rearrange("q n p -> q (n p)"),
                         ps[0:NTILE, :].bitcast(BF16)[:, 0:size * P]).then_inc(onehotT_ready, 1)

            def rows_gathered(j):
                n, size = GROUPS[j]
                ps = await_fill("ga", j)
                act.copy(G[:, n:n + size, :].rearrange("p n w -> p (n w)"),
                         ps[:, 0:size * TW]).then_inc(gathered, 1)

            def exp(g):
                act.wait_ge(max_ready, g + 1)
                if g >= NP:
                    act.wait_ge(turned, g - NP + 1)
                act.activation(probs[:, g % NP, :], psS[g % NS][:], ACT.Exp, bias=nmax[:, g % 8:g % 8 + 1],
                               scale=1.0).then_inc(probs_ready, 1)

            def copy_turned(g):
                act.wait_ge(turned, g + 1)
                if g >= NP:
                    act.wait_ge(pv_done, g - NP + 1)
                act.copy(probsT[:, g % NP, :], psT[:]).then_inc(turned_act, 1)

            act.dma_start(cst[:], consts).then_inc(consts_loaded, 16)
            with nc.allow_non_contiguous_dma(reason="256 biases, one to a partition"):
                for i, v in enumerate((bq, bk)):
                    act.dma_start(bqk[:, i, :], v.rearrange("(c p) -> p c", p=P)).then_inc(bqk_loaded, 16)
            for n, f in (("q", 0.5), ("k", 1.0), ("v", 1.0)):
                act.wait_ge(w_loaded[n], 16)
                act.mul(W_hi[n][:], W[n][:], f).then_inc(w_hi_ready[n], 1)
            act.wait_ge(bqk_loaded, 32)
            act.mul(bias_qk[:, 0, :], bqk[:, 0, :], 0.5)
            act.mul(bias_qk[:, 1, :], bqk[:, 1, :], 1.0).then_inc(bias_ready, 1)
            act.wait_ge(bias_ready, 1)

            def o_high():
                act.wait_ge(w_loaded["o"], 16)
                act.mul(W_hi["o"][:], W["o"][:], 1.0).then_inc(w_hi_ready["o"], 1)

            def slope_signs():
                act.wait_ge(ssum_ready, 1)
                act.activation(ssgn[:], ssum[:], ACT.Sign).then_inc(ssgn_ready, 1)
                act.wait_ge(gbT_loaded, 32)

            copy_out = {"xt0": xn_turned(0), "xt1": xn_turned(1), "q0": projected("q", 0), "k0": projected("k", 0),
                        "q1": projected("q", 1), "k1": projected("k", 1), "ft": feats_turned, "yt": signs,
                        "oht": onehot_turned, "ga": rows_gathered}
            for s in SLOTS:
                for name, i in fills_at(s - 1):
                    if name in copy_out:
                        copy_out[name](i)
                if 0 <= s < NU:
                    exp(s)
                if 0 <= s - TURN < NU and not on_dve(s - TURN):
                    copy_turned(s - TURN)
                for name, i in steps_at(s):
                    if name == "yn" and i < N_GROUPS - LAST_FEW:
                        normalize_y(i)
                    elif name == "slope_signs":
                        slope_signs()
                    elif name == "high_o":
                        o_high()
            for k, (n0, size) in enumerate(PARTS):
                act.wait_ge(c_ready, k + 1)
                for n in range(n0, n0 + size):
                    act.activation(rows_b[:, n, :], x1[:, n, :], ACT.Identity, bias=c0[:, n:n + 1],
                                   scale=c1[:, n:n + 1]).then_inc(rows_ready, 1)

        @block.vector
        def _(dve):
            chain = Chain(dve, dve_chain)

            def await_fill(name, i):
                dve.wait_ge(filled[bank_of(name, i)], filled_count(name, i))
                return psX[bank_of(name, i)]

            def aggregate(mean_var, six, count, done):
                for t in range(count):
                    ins = dve.bn_aggr(mean_var(t), six[:, t, :])
                ins.then_inc(done, 1)

            def x_statistics(i):
                return lambda b: x_statistics_of(b, i)

            def x_statistics_of(b, i):
                if b == 0 and i == 0:
                    dve.wait_ge(x_first_loaded, 16)
                else:
                    dve.wait_ge(x_loaded, 16 * (b + 1))
                for t in (2 * i, 2 * i + 1):
                    ins = dve.bn_stats(st6[:, t, :], x_in[:, T * b + t, :])
                if i == 1:
                    chain(ins)
                    aggregate(lambda t: mvx[:, t, :], st6, T, x_stats)

            def x_norm(i):
                return lambda b: x_norm_of(b, i)

            def x_norm_of(b, i):
                dve.wait_ge(x_rstd, b + 1)
                for t in (2 * i, 2 * i + 1):
                    ins = dve.tensor_scalar(xn[:, t, :], x_in[:, T * b + t, :], mvx[:, t, 0:1],
                                            rx[:, t:t + 1], ALU.subtract, ALU.mult)
                ins.then_inc(xn_ready, 1)

            def xn_low(c):
                def step(b):
                    ps = await_fill(f"xt{c}", b)
                    dve.wait_ge(xnT_hi_ready, 2 * b + c + 1)
                    dve.tensor_tensor(xnT_lo[:, c, :], ps[:], xnT_hi[:, c, :], ALU.subtract).then_inc(xnT_ready, 1)
                return step

            def projected_low(name, m):
                def step(b):
                    ps = await_fill(f"{name}{m}", b)
                    i, hi, lo = (0, q_hi, q_lo) if name == "q" else (1, k_hi, k_lo)
                    dve.wait_ge(qk_hi_ready, 4 * b + 2 * m + i + 1)
                    dve.scalar_tensor_tensor(out=lo[:, b % 2, m, :], in0=ps[:], scalar=bias_qk[:, i, m:m + 1],
                                             in1=hi[:, b % 2, m, :], op0=ALU.add,
                                             op1=ALU.subtract).then_inc(qk_ready, 1)
                return step

            def values(name, t0):
                def step(b):
                    ps = await_fill(name, b)
                    for t in (t0, t0 + 1):
                        ins = dve.tensor_tensor(
                            V[:, b % 2, t, :, 0:DH],
                            ps[:, (t - t0) * F:(t - t0 + 1) * F].rearrange("p (h d) -> p h d", h=H),
                            bv_rows[:].rearrange("p (h d) -> p h d", h=H), ALU.add)
                    ins.then_inc(v_ready, 1)
                return step

            def row_max(g):
                dve.wait_ge(scores_ready, g + 1)
                dve.tensor_reduce(nmax[:, g % 8:g % 8 + 1], psS[g % NS][:], AX.X, ALU.max,
                                  negate=True).then_inc(max_ready, 1)

            def copy_turned(g):
                dve.wait_ge(turned, g + 1)
                if g >= NP:
                    dve.wait_ge(pv_done, g - NP + 1)
                dve.tensor_copy(probsT[:, g % NP, :], psT[:]).then_inc(turned_dve, 1)

            def head_norm(n):
                dve.wait_ge(pv_done, H * n + H)
                o = psV[n % 2][:, 0:H * (DH + 1)].rearrange("p (h d) -> p h d", h=H)
                chain(dve.reciprocal(rsum[:, n % 2, :], o[:, :, DH]))
                at = next(n - n0 for n0, size in GROUPS if n0 <= n < n0 + size)
                dve.tensor_tensor(feats[:, at, :].rearrange("p (h d) -> p h d", h=H), o[:, :, 0:DH],
                                  rsum[:, n % 2, :].unsqueeze(2).broadcast_to([P, H, DH]),
                                  ALU.mult).then_inc(feats_ready, 1)

            def feats_low(j):
                size = GROUPS[j][1]
                ps = await_fill("ft", j)
                dve.wait_ge(featsT_hi_ready, j + 1)
                dve.tensor_tensor(featsT_lo[:, 0:size].rearrange("p t c q -> p (t c q)"), ps[:, 0:size * F],
                                  featsT_hi[:, 0:size].rearrange("p t c q -> p (t c q)"),
                                  ALU.subtract).then_inc(featsT_ready, 1)

            def attn_copy(j):
                size = GROUPS[j][1]
                ps = await_fill("o", j)
                if j >= 1:
                    dve.wait_ge(x1_ready, j)
                dve.tensor_tensor(attn[:, 0:size, :], ps[:, 0:size * F].rearrange("p (t f) -> p t f", t=size),
                                  bo_rows[:].unsqueeze(1).broadcast_to([P, size, F]),
                                  ALU.add).then_inc(o_copied, 1)

            def attn_statistics(j):
                n, size = GROUPS[j]
                dve.wait_ge(o_copied, j + 1)
                for t in range(size):
                    ins = dve.bn_stats(st6a[:, t, :], attn[:, t, :])
                chain(ins)
                aggregate(lambda t: mva[:, n + t, :], st6a, size, a_stats)

            def residual(j):
                n, size = GROUPS[j]
                dve.wait_ge(a_rstd, j + 1)
                for i in range(size):
                    ins = dve.scalar_tensor_tensor(out=x1[:, n + i, :], in0=attn[:, i, :],
                                                   scalar=ra[:, n + i:n + i + 1], in1=x_in[:, n + i, :],
                                                   op0=ALU.mult, op1=ALU.add)
                ins.then_inc(x1_ready, 1)

            def x1_statistics(j):
                n, size = GROUPS[j]
                dve.wait_ge(x1_ready, j + 1)
                for t in range(size):
                    ins = dve.bn_stats(st61[:, t, :], x1[:, n + t, :])
                chain(ins)
                aggregate(lambda t: mv1[:, n + t, :], st61, size, x1_stats)

            def normalize_last_y(j):
                n, size = GROUPS[j]
                dve.wait_ge(x1_scale, j + 1)
                dve.wait_ge(picked, j - 1)
                dve.wait_ge(yn_ready, j)
                for i in range(size):
                    ins = dve.tensor_scalar(yn[:, j % 2, i, :], x1[:, n + i, :], mv1[:, n + i, 0:1],
                                            r12[:, n + i:n + i + 1], ALU.subtract, ALU.mult)
                ins.then_inc(yn_ready, 1)

            def choose(j):
                n, size = GROUPS[j]
                ps = await_fill("key", j)
                ks = ps[:, 0:size * NTILE].rearrange("p (t n) -> p t n", t=size)
                chain(dve.tensor_reduce(kmax[:, 0:size], ks, AX.X, ALU.max))
                dve.tensor_tensor(onehot[:, n:n + size, :], ks,
                                  kmax[:, 0:size].unsqueeze(2).broadcast_to([P, size, NTILE]),
                                  ALU.is_equal).then_inc(onehot_ready, 1)
                dve.wait_ge(onehot_ready, j + 1)
                dve.tensor_scalar(far[:, j % 2, 0:size, :], onehot[:, n:n + size, :], -2 * FAR, FAR,
                                  ALU.mult, ALU.add)

            def picked_features(j):
                n, size = GROUPS[j]
                dve.wait_ge(picked, j + 1)
                dve.tensor_reduce(nsl[:, n:n + size, :],
                                  pick[:, j % 2, 0:size, :].rearrange("p t (n j) -> p t j n", j=DS), AX.X, ALU.add).then_inc(nsl_ready, 1)

            def extremes(j):
                n, size = GROUPS[j]
                r = slice(n, n + size)
                dve.wait_ge(nsl_ready, j + 1)
                dve.wait_ge(gathered, j + 1)
                chain(dve.tensor_tensor(xsl[:, r, :], nsl[:, r, :], G[:, r, TBE:TBE + DS], ALU.mult))
                chain(dve.tensor_tensor(xsl[:, r, :], xsl[:, r, :], G[:, r, TBT:TBT + DS], ALU.add))
                dve.tensor_reduce(tmn[:, 0, 0:size], xsl[:, r, :], AX.X, ALU.min)
                chain(dve.tensor_reduce(tmn[:, 1, 0:size], xsl[:, r, :], AX.X, ALU.max, negate=True))
                for t in range(size):
                    for e in range(2):
                        ins = dve.scalar_tensor_tensor(out=acc[:, e, :], in0=far[:, j % 2, t, :],
                                                       scalar=tmn[:, e, t:t + 1], in1=acc[:, e, :],
                                                       op0=ALU.max, op1=ALU.min)
                    if n + t < NT - 1:
                        chain(ins)
                    else:
                        ins.then_inc(acc_ready, 1)

            def low_part(name):
                dve.wait_ge(w_loaded[name], 16)
                dve.wait_ge(w_hi_ready[name], 1)
                dve.scalar_tensor_tensor(out=W_lo[name][:].rearrange("p c f -> p (c f)"),
                                         in0=W[name][:].rearrange("p c f -> p (c f)"),
                                         scalar=0.5 if name == "q" else 1.0,
                                         in1=W_hi[name][:].rearrange("p c f -> p (c f)"),
                                         op0=ALU.mult, op1=ALU.subtract).then_inc(w_lo_ready[name], 1)

            def await_biases():
                dve.wait_ge(bias_ready, 1)
                dve.wait_ge(bv_loaded, 16)

            def route_signs():
                dve.wait_ge(slp_loaded, 16)
                dve.tensor_reduce(ssum[:], slp[:], AX.X, ALU.add).then_inc(ssum_ready, 1)
                dve.wait_ge(consts_loaded, 16)
                dve.tensor_copy(ident_b[:], ident).then_inc(ident_b_ready, 1)
                dve.wait_ge(bo_loaded, 16)

            def route_matrix():
                dve.tensor_copy(tie_b[:], tie)
                dve.memset(ones_b[:], 1.0)
                dve.wait_ge(ssgn_ready, 1)
                for c in range(KC):
                    ins = dve.tensor_scalar(route[:, c, :], rmask[:, c, :], ssgn[:, c:c + 1], None, ALU.mult)
                ins.then_inc(route_ready, 1)

            dve.memset(acc[:], FAR)
            copy_out = {"xt0": xn_low(0), "xt1": xn_low(1),
                        "q0": projected_low("q", 0), "k0": projected_low("k", 0),
                        "q1": projected_low("q", 1), "k1": projected_low("k", 1), "va": values("va", 0),
                        "vb": values("vb", 2), "ft": feats_low, "o": attn_copy, "key": choose}
            steps = {"heads": head_norm, "stats": attn_statistics, "residual": residual, "x1_stats": x1_statistics,
                     "picked": picked_features, "extremes": extremes, "x_stats0": x_statistics(0),
                     "x_stats1": x_statistics(1), "x_norm0": x_norm(0), "x_norm1": x_norm(1)}
            for s in SLOTS:
                if 0 <= s < NU:
                    row_max(s)
                for name, i in fills_at(s - 1):
                    if name in copy_out:
                        copy_out[name](i)
                if 0 <= s - TURN < NU and on_dve(s - TURN):
                    copy_turned(s - TURN)
                for name, i in steps_at(s):
                    if name in steps:
                        steps[name](i)
                    elif name == "yn" and i >= N_GROUPS - LAST_FEW:
                        normalize_last_y(i)
                    elif name.startswith("low_"):
                        low_part(name[-1])
                    elif name == "biases":
                        await_biases()
                    elif name == "route_signs":
                        route_signs()
                    elif name == "route":
                        route_matrix()

            dve.wait_ge(accT_ready, 1)
            chain(dve.tensor_reduce(tmm[:], psT[0:NTILE, 0:2 * P].rearrange("p (e n) -> p e n", e=2),
                                    AX.X, ALU.min))
            chain(dve.tensor_copy(tmm_b[:, 0, :], tmm[:]))
            chain(dve.tensor_tensor(tmm_rest[:], tmm[:], tmm_b[:, 0, :], ALU.subtract))
            chain(dve.tensor_copy(tmm_b[:, 1, :], tmm_rest[:]))
            dve.tensor_tensor(tmm_b[:, 2, :], tmm_rest[:], tmm_b[:, 1, :], ALU.subtract).then_inc(tmm_ready, 1)
            dve.wait_ge(scales_ready, N_GROUPS - N_LATE + 1)
            dve.scalar_tensor_tensor(out=sq[:], in0=nsl[:], scalar=2.0,
                                     in1=sy[:].unsqueeze(2).broadcast_to([P, NT, DS]), op0=ALU.mult, op1=ALU.mult)
            dve.wait_ge(lohi_filled, 1)
            chain(dve.tensor_reduce(lohi[:], psS[0][:, 0:6 * NT].rearrange("p (n k e) -> p n e k", k=3, e=2),
                                    AX.X, ALU.add))
            chain(dve.scalar_tensor_tensor(out=rden[:], in0=lohi[:, :, 1], scalar=-1.0,
                                           in1=lohi[:, :, 0], op0=ALU.mult, op1=ALU.subtract))
            chain(dve.tensor_scalar(rden[:], rden[:], 1e-8, 1.0 / GRID, ALU.add, ALU.mult))
            dve.reciprocal(rden[:], rden[:])
            chain(dve.tensor_tensor(u16[:], xsl[:], lohi[:, :, 0].unsqueeze(2).broadcast_to([P, NT, DS]),
                                    ALU.subtract))
            chain(dve.tensor_tensor(u16[:], u16[:], rden[:].unsqueeze(2).broadcast_to([P, NT, DS]), ALU.mult))
            chain(dve.tensor_scalar(u16[:], u16[:], 0.0, GRID * BELOW_ONE, ALU.max, ALU.min))
            half = GRID // 2
            bit_at = chain.mark(dve.tensor_scalar(bit[:, half.bit_length() % 2], u16[:], float(half), None,
                                                  ALU.is_ge))
            copied_at = bit_at
            while half:
                now = bit[:, half.bit_length() % 2]

                def halve(first):
                    pieces = G[:, :, first:first + DS * GRID].rearrange("p n (j g) -> p n j g", j=DS)
                    return dve.copy_predicated(pieces[:, :, :, 0:half],
                                               now.bitcast(I32).unsqueeze(3).broadcast_to([P, NT, DS, half]),
                                               pieces[:, :, :, half:2 * half])

                chain.after(bit_at)
                rest_at = chain.mark(dve.scalar_tensor_tensor(out=u16[:], in0=now, scalar=-float(half), in1=u16[:],
                                                              op0=ALU.mult, op1=ALU.add))
                chain.mark(halve(TG))
                if half > 1:
                    chain.after(rest_at)
                    bit_at = chain.mark(dve.tensor_scalar(bit[:, (half // 2).bit_length() % 2], u16[:],
                                                          float(half // 2), None, ALU.is_ge))
                chain.after(copied_at)
                copied_at = chain.mark(halve(TS))
                half //= 2
            chain.after(copied_at)
            base = G[:, :, TG:TG + DS * GRID].rearrange("p n (j g) -> p n j g", j=DS)[:, :, :, 0]
            slope = G[:, :, TS:TS + DS * GRID].rearrange("p n (j g) -> p n j g", j=DS)[:, :, :, 0]
            chain(dve.tensor_tensor(delta[:], slope, u16[:], ALU.mult))
            chain(dve.tensor_tensor(delta[:], delta[:], base, ALU.add))
            chain(dve.tensor_tensor(delta[:], delta[:], G[:, :, TGA:TGA + 1].broadcast_to([P, NT, DS]), ALU.mult))
            sum_at = chain.mark(dve.tensor_tensor(sq[:], sq[:], delta[:], ALU.add))
            s1_at = chain.mark(dve.tensor_reduce(s1[:], delta[:], AX.X, ALU.add))
            chain.after(sum_at)
            sq_at = chain.mark(dve.tensor_tensor(sq[:], sq[:], delta[:], ALU.mult))
            chain.after(s1_at)
            dve.scalar_tensor_tensor(out=c0[:], in0=s1[:], scalar=1.0 / F ** 2, in1=s1[:],
                                     op0=ALU.mult, op1=ALU.mult)
            chain.after(sq_at)
            s2_at = chain.mark(dve.tensor_reduce(s2[:], sq[:], AX.X, ALU.add))
            dve.scalar_tensor_tensor(out=ym[:], in0=s1[:], scalar=-1.0 / F, in1=ym[:], op0=ALU.mult, op1=ALU.add)
            chain.after(s2_at)
            chain(dve.scalar_tensor_tensor(out=s2[:], in0=s2[:], scalar=1.0 / F, in1=vy[:],
                                           op0=ALU.mult, op1=ALU.add))
            dve.scalar_tensor_tensor(out=s2[:], in0=s2[:], scalar=EPS, in1=c0[:],
                                     op0=ALU.add, op1=ALU.subtract).then_inc(var3_ready, 1)
            by_dve = NT - BY_POOL
            for n in range(SPREAD_FIRST):
                spread(dve, n).then_inc(put_dve, 1)
            for k, (n0, size) in enumerate(PARTS):
                r = slice(n0, n0 + size)
                dve.wait_ge(r3_ready, k + 1)
                dve.tensor_tensor(c1[:, r], r1[:, r], r3[:, r], ALU.mult)
                chain(dve.tensor_tensor(c0[:, r], ym[:, r], r3[:, r], ALU.mult))
                dve.tensor_scalar(c1[:, r], c1[:, r], 1.0, None, ALU.add)
                dve.tensor_tensor(c0[:, r], c0[:, r], shift[:, r], ALU.subtract).then_inc(c_ready, 1)
                for n in range(max(n0, SPREAD_FIRST), min(n0 + size, by_dve)):
                    spread(dve, n).then_inc(put_dve, 1)
            for n in range(NT):
                if n < by_dve:
                    dve.wait_ge(put_dve, n + 1)
                else:
                    dve.wait_ge(put_ready, n + 1 - by_dve)
                dve.wait_ge(rows_ready, n + 1)
                ins = dve.scalar_tensor_tensor(out=res[:, n, :], in0=put[:, n, :], scalar=r3[:, n:n + 1],
                                               in1=rows_b[:, n, :], op0=ALU.mult, op1=ALU.add)
                if n % 2:
                    ins.then_inc(res_ready, 1)

        @block.tensor
        def _(pe):
            def fill(name, emit, source):
                def step(i):
                    at = ORDER[name, i]
                    if at >= NX:
                        pe.wait_ge(*copied_out(FILLS[at - NX][1], FILLS[at - NX][2]))
                    pe.wait_ge(*source(i))
                    emit(psX[at % NX], i).then_inc(filled[at % NX], 1)
                return step

            def turn_xn(c):
                def emit(ps, b):
                    for t in range(T):
                        ins = pe.transpose(ps[:, t * P:(t + 1) * P], xn[:, t, c * P:(c + 1) * P], ident)
                    return ins
                return emit

            def parts(out, a_hi, a_lo, b_hi, b_lo, first, last):
                pe.matmul(out, a_hi, b_lo, start=first, stop=False)
                pe.matmul(out, a_lo, b_hi, start=False, stop=False)
                return pe.matmul(out, a_hi, b_hi, start=False, stop=last)

            def project(name, m):
                cols = slice(m * P, (m + 1) * P)

                def emit(ps, b):
                    if b == 0 and m == 0:
                        pe.wait_ge(w_lo_ready[name], 1)
                    for c in range(KC):
                        pe.wait_ge(xnT_ready, 2 * b + c + 1)
                        ins = parts(ps[:], W_hi[name][:, c, cols], W_lo[name][:, c, cols],
                                    xnT_hi[:, c, :], xnT_lo[:, c, :], c == 0, c == KC - 1)
                    return ins
                return emit

            def project_v(t0):
                def emit(ps, b):
                    if b == 0 and t0 == 0:
                        pe.wait_ge(w_lo_ready["v"], 1)
                    for t in (t0, t0 + 1):
                        rows = slice(t * P, (t + 1) * P)
                        for c in range(KC):
                            ins = parts(ps[:, (t - t0) * F:(t - t0 + 1) * F], xnT_hi[:, c, rows],
                                        xnT_lo[:, c, rows], W_hi["v"][:, c, :], W_lo["v"][:, c, :],
                                        c == 0, c == KC - 1)
                    return ins
                return emit

            def turn_feats(ps, j):
                for i in range(GROUPS[j][1]):
                    for c in range(KC):
                        ins = pe.transpose(ps[:, i * F + c * P:i * F + (c + 1) * P],
                                           feats[:, i, c * P:(c + 1) * P], ident)
                return ins

            def project_o(ps, j):
                if j == 0:
                    pe.wait_ge(w_lo_ready["o"], 1)
                for i in range(GROUPS[j][1]):
                    for c in range(KC):
                        ins = parts(ps[:, i * F:(i + 1) * F], featsT_hi[:, i, c, :], featsT_lo[:, i, c, :],
                                    W_hi["o"][:, c, :], W_lo["o"][:, c, :], c == 0, c == KC - 1)
                return ins

            def turn_yn(ps, j):
                for c in range(KC):
                    for i in range(GROUPS[j][1]):
                        ins = pe.transpose(ps[:, (c * GT + i) * P:(c * GT + i + 1) * P],
                                           yn[:, j % 2, i, c * P:(c + 1) * P], ident)
                return ins

            def key_sums(ps, j):
                if j == 0:
                    pe.wait_ge(route_ready, 1)
                for i in range(GROUPS[j][1]):
                    keys = ps[:, i * NTILE:(i + 1) * NTILE]
                    pe.matmul(keys, ones_b[:], tie_b[:], start=True, stop=False)
                    for c in range(KC):
                        ins = pe.matmul(keys, signT[:, c, i * P:(i + 1) * P], route[:, c, :],
                                        start=False, stop=(c == KC - 1))
                return ins

            def turn_onehot(ps, j):
                n, size = GROUPS[j]
                if j == 0:
                    pe.wait_ge(ident_b_ready, 1)
                for i in range(size):
                    ins = pe.transpose(ps[0:NTILE, :].bitcast(BF16)[:, i * P:(i + 1) * P],
                                       onehot[:, n + i, :], ident_b[:])
                return ins

            def gather_rows(ps, j):
                n, size = GROUPS[j]
                if j == 0:
                    pe.wait_ge(table_ready, 1)
                for i in range(size):
                    for k in (2, 1, 0):
                        ins = pe.matmul(ps[:, i * TW:(i + 1) * TW], onehotT[:, n + i, :], table_b[k][:],
                                        start=(k == 2), stop=(k == 0))
                return ins

            def scores(g):
                b, h, t = g // UB, g % H, g % UB // H
                if t == 0 and h % 2 == 0:
                    pe.wait_ge(qk_ready, 4 * b + h + 2)
                if g >= NS:
                    pe.wait_ge(probs_ready, g - NS + 1)
                rows = slice(DH * (h % 2), DH * (h % 2) + DH)
                m, qs = h // 2, slice(t * P, (t + 1) * P)
                parts(psS[g % NS][:], q_hi[rows, b % 2, m, qs], q_lo[rows, b % 2, m, qs],
                      k_hi[rows, b % 2, m, :], k_lo[rows, b % 2, m, :], True, True).then_inc(scores_ready, 1)

            def copied(g):
                by_dve = sum(on_dve(i) for i in range(g + 1))
                if on_dve(g):
                    pe.wait_ge(turned_dve, by_dve)
                else:
                    pe.wait_ge(turned_act, g + 1 - by_dve)

            def transposes(g):
                pe.wait_ge(probs_ready, g + 1)
                if g >= 1:
                    copied(g - 1)
                for k in range(T):
                    ins = pe.transpose(psT[:, k * P:(k + 1) * P], probs[:, g % NP, k * P:(k + 1) * P], ident)
                ins.then_inc(turned, 1)

            def weighted(g):
                b, h, n = g // UB, g % H, g // H
                copied(g)
                if g % UB == 0:
                    pe.wait_ge(v_ready, 2 * b + 2)
                if h == 0 and n >= 2:
                    pe.wait_ge(feats_ready, n - 1)
                for k in range(T):
                    ins = pe.matmul(psV[n % 2][:, h * (DH + 1):(h + 1) * (DH + 1)],
                                    probsT[:, g % NP, k * P:(k + 1) * P], V[:, b % 2, k, h, :],
                                    start=(k == 0), stop=(k == T - 1))
                ins.then_inc(pv_done, 1)

            def by_batch(s, per):
                return lambda b: (s, per * (b + 1))

            def by_group(s):
                return lambda j: (s, j + 1)

            fills = {
                "xt0": fill("xt0", turn_xn(0), by_batch(xn_ready, 2)),
                "xt1": fill("xt1", turn_xn(1), by_batch(xn_ready, 2)),
                "va": fill("va", project_v(0), by_batch(xnT_ready, 2)),
                "vb": fill("vb", project_v(2), by_batch(xnT_ready, 2)),
                "ft": fill("ft", turn_feats, lambda j: (feats_ready, sum(GROUPS[j]))),
                "o": fill("o", project_o, by_group(featsT_ready)),
                "yt": fill("yt", turn_yn, by_group(yn_ready)),
                "key": fill("key", key_sums, by_group(sign_ready)),
                "oht": fill("oht", turn_onehot, by_group(onehot_ready)),
                "ga": fill("ga", gather_rows, by_group(onehotT_ready)),
            }
            for m in range(KC):
                for name in "qk":
                    fills[f"{name}{m}"] = fill(f"{name}{m}", project(name, m), lambda b: (xnT_ready, 2 * b + 1))

            pe.wait_ge(consts_loaded, 16)
            for _ in range(WARM_UP):
                pe.transpose(psT[:, 0:P], ident, ident)
            pe.wait_ge(ones_set, 1)
            for s in SLOTS:
                if 0 <= s < NU:
                    scores(s)
                if 0 <= s - WEIGH < NU:
                    weighted(s - WEIGH)
                if 0 <= s - TURN < NU:
                    transposes(s - TURN)
                for name, i in fills_at(s):
                    fills[name](i)

            pe.wait_ge(acc_ready, 1)
            for e in range(2):
                ins = pe.transpose(psT[0:NTILE, e * P:(e + 1) * P], acc[:, e, :], ident)
            ins.then_inc(accT_ready, 1)
            pe.wait_ge(tmm_ready, 1)
            for n in range(NT):
                ins = pe.matmul(psS[0][:, 6 * n:6 * n + 6], onehotT[:, n, :],
                                tmm_b[:].rearrange("q k e -> q (k e)"),
                                start=True, stop=True)
            ins.then_inc(lohi_filled, 1)


_INS = ["L0_attn_x", "L0_attn_Wq", "L0_attn_bq", "L0_attn_Wk", "L0_attn_bk", "L0_attn_Wv", "L0_attn_bv",
        "L0_attn_Wo", "L0_attn_bo", "L0_ffn_ln_gamma", "L0_ffn_ln_beta", "L0_ffn_spline_bases",
        "L0_ffn_spline_slopes", "L0_ffn_output_scale"]


def shape_constants(np):
    c = np.zeros((P, CW), np.float32)
    c[:, 0:P] = np.eye(P)
    feature = np.arange(KC)[None, :, None] * P + np.arange(P)[:, None, None]
    tile = np.arange(NTILE)[None, None, :]
    mask = (1024 * (feature // (F // NCL) == tile // (NTILE // NCL)) + 8 * (feature // DS == tile))
    c[:, P:P + KC * NTILE] = mask.reshape(P, KC * NTILE)
    n = np.arange(NTILE)
    c[0, P + KC * NTILE:] = 128 * (NCL - 1 - n // NCL)
    c[1, P + KC * NTILE:] = NCL - 1 - n % NCL
    return c


def kernel(**inputs):
    import numpy as _np
    import concourse.bacc as _bacc
    from concourse.bass_utils import run_bass_kernel_spmd as _run

    nc = _bacc.Bacc("TRN2", target_bir_lowering=False, num_devices=1)
    arrays = {f"in_{n}": _np.ascontiguousarray(inputs[n]) for n in _INS}
    arrays["in_shape_constants"] = shape_constants(_np)
    args = [nc.dram_tensor(n, a.shape, mybir.dt.from_np(a.dtype), kind="ExternalInput").ap()
            for n, a in arrays.items()]
    args.append(nc.dram_tensor("out_dram", (NB, SEQ, F), F32, kind="ExternalOutput").ap())
    sandwich(nc, *args)
    r = _run(nc, [arrays], core_ids=[0])
    return r.results[0]["out_dram"]
```
